# Optimizing a Trainium2 kernel written in Bass

```python
import numpy as np
import jax
import jax.numpy as jnp

def _softmax(x, axis=-1):
    return jax.nn.softmax(x, axis=axis)

def _gelu(x):
    return jax.nn.gelu(x, approximate=True)

def _silu(x):
    return jax.nn.silu(x)

def _sigmoid(x):
    return jax.nn.sigmoid(x)

def _layernorm(x, axis=-1, eps=1e-05):
    m = jnp.mean(x, axis=axis, keepdims=True)
    v = jnp.var(x, axis=axis, keepdims=True)
    return (x - m) / jnp.sqrt(v + eps)

def _scatter_add(tgt, idx, src, axis=0):
    return tgt.at[idx].add(src)

def _segment_sum(src, seg, n):
    return jax.ops.segment_sum(src, seg, n)
kernel_name = 'mk_macaron_d2_jaxref_r4_189b5a'

def setup_inputs(seed: int=0):
    np.random.seed(seed)
    _w = jnp.asarray

    def _L0_attn_setup():
        import jax, jax.numpy as jnp
        import numpy as np
        B, T, C = (2, 512, 256)
        H = 16
        HS = C // H
        key = jax.random.key(seed)
        k1, k2, k3 = jax.random.split(key, 3)
        x = jax.random.normal(k1, (B, T, C), dtype=jnp.float32)
        w_qkv = jax.random.normal(k2, (3 * C, C), dtype=jnp.float32) * C ** (-0.5)
        w_proj = jax.random.normal(k3, (C, C), dtype=jnp.float32) * C ** (-0.5)
        b_proj = jnp.zeros((C,), dtype=jnp.float32)
        return {'x': x, 'w_qkv': w_qkv, 'w_proj': w_proj, 'b_proj': b_proj}
    _L0_attn_in = _L0_attn_setup()

    def _L0_ffn_setup():
        import jax, jax.numpy as jnp
        import numpy as np
        from jax import lax
        T, B, I, M, O = (64, 64, 256, 256, 256)

        def _xavier(key, shape):
            fan_out, fan_in = shape
            limit = float(np.sqrt(6.0 / (fan_in + fan_out)))
            return jax.random.uniform(key, shape, jnp.float32, -limit, limit)
        key = jax.random.key(seed)
        ks = jax.random.split(key, 9)
        x = jax.random.normal(ks[0], (T, B, I), jnp.float32)
        return {'x': x, 'wf': _xavier(ks[1], (M, I)), 'uf': _xavier(ks[2], (M, M)), 'bf': jnp.zeros((M,), jnp.float32), 'wi': _xavier(ks[3], (M, I)), 'ui': _xavier(ks[4], (M, M)), 'bi': jnp.zeros((M,), jnp.float32), 'wc': _xavier(ks[5], (M, I)), 'uc': _xavier(ks[6], (M, M)), 'bc': jnp.zeros((M,), jnp.float32), 'wo': _xavier(ks[7], (O, I)), 'uo': _xavier(ks[8], (O, M)), 'bo': jnp.zeros((O,), jnp.float32), 'in_c': jnp.zeros((M,), jnp.float32)}
    _L0_ffn_in = _L0_ffn_setup()

    def _L1_attn_setup():
        import jax, jax.numpy as jnp
        import numpy as np
        D_MODEL = 256
        D_STATE = 128
        HEAD_DIM = 64
        EXPAND = 2
        K = 4
        N_GROUPS = 1
        D_INNER = EXPAND * D_MODEL
        N_HEADS = D_INNER // HEAD_DIM
        D_PROJ = 2 * D_INNER + 2 * N_GROUPS * D_STATE + N_HEADS
        EPS = 1e-06

        def _rmsnorm(x, w):
            return x * jax.lax.rsqrt(jnp.mean(x * x, axis=-1, keepdims=True) + EPS) * w
        key = jax.random.key(seed)
        ks = jax.random.split(key, 8)
        B, L = (2, 512)
        x = jax.random.normal(ks[0], (B, L, D_MODEL), jnp.float32)
        norm_w = jnp.ones((D_MODEL,), jnp.float32)
        in_proj_w = jax.random.normal(ks[1], (D_PROJ, D_MODEL), jnp.float32) / np.sqrt(D_MODEL).astype(np.float32)
        conv_w = jax.random.normal(ks[2], (D_INNER, K), jnp.float32) / np.sqrt(K).astype(np.float32)
        conv_b = jnp.zeros((D_INNER,), jnp.float32)
        A_log = jnp.log(jax.random.uniform(ks[3], (N_HEADS,), jnp.float32) * 15.0 + 1.0)
        D = jnp.ones((N_HEADS,), jnp.float32)
        dt_bias = jnp.log(jax.random.uniform(ks[4], (N_HEADS,), jnp.float32) * 0.099 + 0.001)
        out_proj_w = jax.random.normal(ks[5], (D_MODEL, D_INNER), jnp.float32) / np.sqrt(D_INNER).astype(np.float32)
        return dict(x=x, norm_w=norm_w, in_proj_w=in_proj_w, conv_w=conv_w, conv_b=conv_b, A_log=A_log, D=D, dt_bias=dt_bias, out_proj_w=out_proj_w)
    _L1_attn_in = _L1_attn_setup()

    def _L1_ffn_setup():
        import jax, jax.numpy as jnp
        import numpy as np
        TOP_K = 2
        key = jax.random.key(seed)
        k1, k2, k3 = jax.random.split(key, 3)
        B, S, H, E = (4, 512, 256, 8)
        x = jax.random.normal(k1, (B, S, H), dtype=jnp.float32)
        gate_w = jax.random.normal(k2, (E, H), dtype=jnp.float32) / np.sqrt(H)
        gate_b = jnp.zeros((E,), dtype=jnp.float32)
        expert_w = jax.random.normal(k3, (E, H, H), dtype=jnp.float32) / np.sqrt(H)
        expert_b = jnp.zeros((E, H), dtype=jnp.float32)
        return {'x': x, 'gate_w': gate_w, 'gate_b': gate_b, 'expert_w': expert_w, 'expert_b': expert_b}
    _L1_ffn_in = _L1_ffn_setup()
    _d = {'L0_attn_x': _L0_attn_in['x'], 'L0_attn_w_qkv': _L0_attn_in['w_qkv'], 'L0_attn_w_proj': _L0_attn_in['w_proj'], 'L0_attn_b_proj': _L0_attn_in['b_proj'], 'L0_ffn_wf': _L0_ffn_in['wf'], 'L0_ffn_uf': _L0_ffn_in['uf'], 'L0_ffn_bf': _L0_ffn_in['bf'], 'L0_ffn_wi': _L0_ffn_in['wi'], 'L0_ffn_ui': _L0_ffn_in['ui'], 'L0_ffn_bi': _L0_ffn_in['bi'], 'L0_ffn_wc': _L0_ffn_in['wc'], 'L0_ffn_uc': _L0_ffn_in['uc'], 'L0_ffn_bc': _L0_ffn_in['bc'], 'L0_ffn_wo': _L0_ffn_in['wo'], 'L0_ffn_uo': _L0_ffn_in['uo'], 'L0_ffn_bo': _L0_ffn_in['bo'], 'L0_ffn_in_c': _L0_ffn_in['in_c'], 'L1_attn_norm_w': _L1_attn_in['norm_w'], 'L1_attn_in_proj_w': _L1_attn_in['in_proj_w'], 'L1_attn_conv_w': _L1_attn_in['conv_w'], 'L1_attn_conv_b': _L1_attn_in['conv_b'], 'L1_attn_A_log': _L1_attn_in['A_log'], 'L1_attn_D': _L1_attn_in['D'], 'L1_attn_dt_bias': _L1_attn_in['dt_bias'], 'L1_attn_out_proj_w': _L1_attn_in['out_proj_w'], 'L1_ffn_gate_w': _L1_ffn_in['gate_w'], 'L1_ffn_gate_b': _L1_ffn_in['gate_b'], 'L1_ffn_expert_w': _L1_ffn_in['expert_w'], 'L1_ffn_expert_b': _L1_ffn_in['expert_b']}
    _x0 = _d['L0_attn_x']
    _d['L0_attn_x'] = jax.random.normal(jax.random.fold_in(jax.random.key(seed), 1), (4, 1024, 256), dtype=_x0.dtype)
    del _x0
    return _d

def reference(L0_attn_x, L0_attn_w_qkv, L0_attn_w_proj, L0_attn_b_proj, L0_ffn_wf, L0_ffn_uf, L0_ffn_bf, L0_ffn_wi, L0_ffn_ui, L0_ffn_bi, L0_ffn_wc, L0_ffn_uc, L0_ffn_bc, L0_ffn_wo, L0_ffn_uo, L0_ffn_bo, L0_ffn_in_c, L1_attn_norm_w, L1_attn_in_proj_w, L1_attn_conv_w, L1_attn_conv_b, L1_attn_A_log, L1_attn_D, L1_attn_dt_bias, L1_attn_out_proj_w, L1_ffn_gate_w, L1_ffn_gate_b, L1_ffn_expert_w, L1_ffn_expert_b):

    def _L0_attn_ref(x, w_qkv, w_proj, b_proj):
        import jax, jax.numpy as jnp
        import numpy as np
        B, T, C = (2, 512, 256)
        H = 16
        HS = C // H
        b, t, c = x.shape
        hs = c // H
        qkv = jnp.einsum('btc,fc->btf', x, w_qkv)
        qkv = qkv.reshape(b, t, 3, H, hs)
        q = jnp.transpose(qkv[:, :, 0], (0, 2, 1, 3))
        k = jnp.transpose(qkv[:, :, 1], (0, 2, 1, 3))
        v = jnp.transpose(qkv[:, :, 2], (0, 2, 1, 3))
        scores = jnp.einsum('bhqd,bhkd->bhqk', q, k) * hs ** (-0.5)
        p = jax.nn.softplus(scores)
        p = p * p
        causal = jnp.tril(jnp.ones((t, t), dtype=p.dtype))
        p = p * causal
        attn = p / (jnp.sum(p, axis=-1, keepdims=True) + 1e-09)
        out = jnp.einsum('bhqk,bhkd->bhqd', attn, v)
        out = jnp.transpose(out, (0, 2, 1, 3)).reshape(b, t, c)
        return jnp.einsum('btc,oc->bto', out, w_proj) + b_proj

    def _L0_ffn_ref(x, wf, uf, bf, wi, ui, bi, wc, uc, bc, wo, uo, bo, in_c):
        import jax, jax.numpy as jnp
        import numpy as np
        from jax import lax
        T, B, I, M, O = (64, 64, 256, 256, 256)

        def _xavier(key, shape):
            fan_out, fan_in = shape
            limit = float(np.sqrt(6.0 / (fan_in + fan_out)))
            return jax.random.uniform(key, shape, jnp.float32, -limit, limit)
        batch = x.shape[1]
        c0 = jnp.broadcast_to(in_c, (batch, in_c.shape[0]))

        def step(c, xt):
            ft = jax.nn.sigmoid(xt @ wf.T + c @ uf.T + bf)
            it = jax.nn.sigmoid(xt @ wi.T + c @ ui.T + bi)
            gt = jnp.tanh(xt @ wc.T + c @ uc.T + bc)
            c = ft * c + it * gt
            return (c, None)
        c_final, _ = lax.scan(step, c0, x)
        h = jnp.tanh(jnp.einsum('tbi,oi->tbo', x, wo) + c_final @ uo.T + bo)
        return h

    def _L1_attn_ref(x, norm_w, in_proj_w, conv_w, conv_b, A_log, D, dt_bias, out_proj_w):
        import jax, jax.numpy as jnp
        import numpy as np
        D_MODEL = 256
        D_STATE = 128
        HEAD_DIM = 64
        EXPAND = 2
        K = 4
        N_GROUPS = 1
        D_INNER = EXPAND * D_MODEL
        N_HEADS = D_INNER // HEAD_DIM
        D_PROJ = 2 * D_INNER + 2 * N_GROUPS * D_STATE + N_HEADS
        EPS = 1e-06

        def _rmsnorm(x, w):
            return x * jax.lax.rsqrt(jnp.mean(x * x, axis=-1, keepdims=True) + EPS) * w
        batch, L, _ = x.shape
        residual = x
        xn = _rmsnorm(x, norm_w)
        proj = jnp.einsum('bld,pd->blp', xn, in_proj_w)
        i = 0
        z = proj[:, :, i:i + D_INNER]
        i += D_INNER
        x_ssm = proj[:, :, i:i + D_INNER]
        i += D_INNER
        bc = N_GROUPS * D_STATE
        Bm = proj[:, :, i:i + bc].reshape(batch, L, N_GROUPS, D_STATE)
        i += bc
        Cm = proj[:, :, i:i + bc].reshape(batch, L, N_GROUPS, D_STATE)
        i += bc
        dt_raw = proj[:, :, i:i + N_HEADS]
        xp = jnp.pad(x_ssm, ((0, 0), (K - 1, 0), (0, 0)))
        x_conv = conv_b
        for k in range(K):
            x_conv = x_conv + xp[:, k:k + L, :] * conv_w[:, k]
        x_conv = jax.nn.silu(x_conv)
        xh = x_conv.reshape(batch, L, N_HEADS, HEAD_DIM)
        dt = jax.nn.softplus(dt_raw + dt_bias)
        dA = jnp.exp(-jnp.exp(A_log) * dt)
        dtx = dt[..., None] * xh
        gidx = jnp.arange(N_HEADS) // (N_HEADS // N_GROUPS)
        Bg = Bm[:, :, gidx, :]
        Cg = Cm[:, :, gidx, :]

        def step(h, inp):
            dA_t, dtx_t, B_t, C_t = inp
            h = h * dA_t[:, :, None, None] + dtx_t[..., None] * B_t[:, :, None, :]
            y_t = jnp.einsum('bhpn,bhn->bhp', h, C_t)
            return (h, y_t)
        h0 = jnp.zeros((batch, N_HEADS, HEAD_DIM, D_STATE), jnp.float32)
        xs = (jnp.swapaxes(dA, 0, 1), jnp.swapaxes(dtx, 0, 1), jnp.swapaxes(Bg, 0, 1), jnp.swapaxes(Cg, 0, 1))
        _, ys = jax.lax.scan(step, h0, xs)
        y = jnp.swapaxes(ys, 0, 1) + D[None, None, :, None] * xh
        y = y.reshape(batch, L, D_INNER) * jax.nn.silu(z)
        return residual + jnp.einsum('bli,di->bld', y, out_proj_w)

    def _L1_ffn_ref(x, gate_w, gate_b, expert_w, expert_b):
        import jax, jax.numpy as jnp
        import numpy as np
        TOP_K = 2
        gates = jax.nn.softmax(jnp.einsum('bsh,eh->bse', x, gate_w) + gate_b, axis=-1)
        top_gates, top_idx = jax.lax.top_k(gates, TOP_K)
        expert_out = jnp.einsum('bsh,eoh->bseo', x, expert_w) + expert_b
        selected = jnp.take_along_axis(expert_out, top_idx[..., None], axis=2)
        return (selected * top_gates[..., None]).sum(axis=2)
    x = L0_attn_x
    x = x + 0.5 * _L0_ffn_ref(_layernorm(x, axis=-1), L0_ffn_wf, L0_ffn_uf, L0_ffn_bf, L0_ffn_wi, L0_ffn_ui, L0_ffn_bi, L0_ffn_wc, L0_ffn_uc, L0_ffn_bc, L0_ffn_wo, L0_ffn_uo, L0_ffn_bo, L0_ffn_in_c)
    x = x + _L0_attn_ref(_layernorm(x, axis=-1), L0_attn_w_qkv, L0_attn_w_proj, L0_attn_b_proj)
    x = x + 0.5 * _L0_ffn_ref(_layernorm(x, axis=-1), L0_ffn_wf, L0_ffn_uf, L0_ffn_bf, L0_ffn_wi, L0_ffn_ui, L0_ffn_bi, L0_ffn_wc, L0_ffn_uc, L0_ffn_bc, L0_ffn_wo, L0_ffn_uo, L0_ffn_bo, L0_ffn_in_c)
    x = x + 0.5 * _L1_ffn_ref(_layernorm(x, axis=-1), L1_ffn_gate_w, L1_ffn_gate_b, L1_ffn_expert_w, L1_ffn_expert_b)
    x = x + _L1_attn_ref(_layernorm(x, axis=-1), L1_attn_norm_w, L1_attn_in_proj_w, L1_attn_conv_w, L1_attn_conv_b, L1_attn_A_log, L1_attn_D, L1_attn_dt_bias, L1_attn_out_proj_w)
    x = x + 0.5 * _L1_ffn_ref(_layernorm(x, axis=-1), L1_ffn_gate_w, L1_ffn_gate_b, L1_ffn_expert_w, L1_ffn_expert_b)
    return x

_drawn_inputs = setup_inputs


def setup_inputs(seed=0):
    import zlib

    import numpy as np

    out = dict(_drawn_inputs(seed))
    spreads = {'L0_attn_b_proj': (0.0, 0.1),
     'L0_ffn_bf': (0.0, 0.488),
     'L0_ffn_bi': (0.0, 0.39),
     'L0_ffn_bc': (0.0, 0.1),
     'L0_ffn_bo': (0.0, 0.1),
     'L0_ffn_in_c': (0.0, 0.1),
     'L1_attn_norm_w': (1.0, 0.2),
     'L1_attn_conv_b': (0.0, 0.1),
     'L1_attn_D': (1.0, 0.549),
     'L1_ffn_gate_b': (0.0, 0.1),
     'L1_ffn_expert_b': (0.0, 0.1)}
    factors = {}
    for name, (base, spread) in spreads.items():
        noise = np.random.default_rng([zlib.crc32(name.encode()), seed]).standard_normal(out[name].shape)
        drawn = base * np.exp(spread * noise) if base else spread * noise
        out[name] = jnp.asarray(drawn.astype(out[name].dtype))
    for name, factor in factors.items():
        out[name] = (out[name] * factor).astype(out[name].dtype)
    return out
```

```python
from contextlib import ExitStack

import numpy as np

import concourse.bass as bass
from concourse import mybir

F32 = mybir.dt.float32
F32R = mybir.dt.float32r
BF16 = mybir.dt.bfloat16
U32 = mybir.dt.uint32
ALU = mybir.AluOpType
ACT = mybir.ActivationFunctionType
AX = mybir.AxisListType

P = 128
B, T, C = 4, 1024, 256
KC = C // P
TILES = B * T // P
PT = T // P
GT = 4
GROUPS = TILES // GT
GN = GT * P
GW = GT * C
BANK = 512
LN_EPS = 1e-5
RING = 4

SIGMOID_SET = "sigmoid_and_others"
EXP_SET = "exp_and_others"
LN_EXP_SET = "natural_log_exp_and_others"
SILU_SET = "silu_and_others"


def f32(ap):
    return ap.bitcast(F32)


def matmul3(pe, out, lhs_hi, lhs_lo, rhs_hi, rhs_lo, ks, first=True, last=True):
    passes = [(l, r, k) for k in ks for l, r in ((lhs_hi, rhs_hi), (lhs_lo, rhs_hi), (lhs_hi, rhs_lo))]
    for n, (l, r, k) in enumerate(passes):
        ins = pe.matmul(out, l(k), r(k), start=first and n == 0, stop=last and n == len(passes) - 1)
    return ins


class Phase(ExitStack):

    def __init__(self, nc):
        super().__init__()
        self.nc, self.semaphores = nc, []

    def sem(self, name):
        self.semaphores.append(self.nc.alloc_semaphore(name=name))
        return self.semaphores[-1]

    def __exit__(self, *error):
        super().__exit__(*error)
        if error[0] is None:
            self.nc.clear_and_free_semaphores(self.semaphores)
            self.nc.all_engine_barrier()


class Norm:

    def __init__(self, nc, sb, sem, psum_t, ident, tag, slots=2):
        self.nc, self.ps, self.ident = nc, psum_t, ident
        self.xn = sb(f"{tag}_xn", [P, slots, GW], F32)
        self.stats = sb(f"{tag}_stats", [P, slots, GT, 6], F32)
        self.mv = sb(f"{tag}_mv", [P, slots, GT, 2], F32)
        self.var = sb(f"{tag}_var", [P, slots, GT], F32)
        self.rstd = sb(f"{tag}_rstd", [P, slots, GT], F32)
        self.power = sb(f"{tag}_power", [P, GT], F32)
        self.xh = sb(f"{tag}_xh", [P, slots, KC, GN], F32R)
        self.xl = sb(f"{tag}_xl", [P, slots, KC, GN], F32R)
        self.power_set = sem(f"{tag}_power_set")
        self.mv_done = sem(f"{tag}_mv_done")
        self.var_done = sem(f"{tag}_var_done")
        self.rstd_done = sem(f"{tag}_rstd_done")
        self.xn_done = sem(f"{tag}_xn_done")
        self.turned = sem(f"{tag}_turned")
        self.xh_done = sem(f"{tag}_xh_done")
        self.xl_done = sem(f"{tag}_xl_done")

    def pool_setup(self, pool):
        pool.memset(self.power[:, :], -0.5).then_inc(self.power_set, 1)
        pool.wait_ge(self.power_set, 1)

    def pool_rstd(self, pool, n, s):
        pool.wait_ge(self.var_done, n + 1)
        pool.tensor_tensor(self.rstd[:, s], self.var[:, s], self.power[:, :], ALU.pow).then_inc(self.rstd_done, 1)

    def dve_stats(self, dve, n, s, x):
        for j in range(GT):
            dve.bn_stats(self.stats[:, s, j], x(j))
        dve.drain()
        for j in range(GT):
            ins = dve.bn_aggr(self.mv[:, s, j], self.stats[:, s, j])
        ins.then_inc(self.mv_done, 1)
        dve.wait_ge(self.mv_done, n + 1)
        if not isinstance(n, int) or n:
            dve.wait_ge(self.rstd_done, n)
        dve.tensor_scalar(self.var[:, s], self.mv[:, s, :, 1], LN_EPS, None, ALU.add).then_inc(self.var_done, 1)

    def dve_apply(self, dve, n, s, x, done=None):
        dve.wait_ge(self.rstd_done, n + 1)
        for j in range(GT):
            ins = dve.tensor_scalar(self.xn[:, s, j * C:(j + 1) * C], x(j), self.mv[:, s, j, 0:1],
                                    self.rstd[:, s, j:j + 1], ALU.subtract, ALU.mult)
        ins.then_inc(done or self.xn_done, 1)

    def pe_turn(self, pe, n, s):
        pe.wait_ge(self.xn_done, n + 1)
        pe.wait_ge(self.xh_done, n)
        pe.wait_ge(self.xl_done, n)
        for k in range(KC):
            for j in range(GT):
                ins = pe.transpose(self.ps[:, k, j * P:(j + 1) * P],
                                   self.xn[:, s, j * C + k * P:j * C + (k + 1) * P], self.ident[:, :])
        ins.then_inc(self.turned, 1)

    def act_hi(self, act, n, s):
        act.wait_ge(self.turned, n + 1)
        act.activation(self.xh[:, s], self.ps[:, :, :], ACT.Copy).then_inc(self.xh_done, 1)

    def dve_lo(self, dve, n, s):
        dve.wait_ge(self.xh_done, n + 1)
        dve.tensor_tensor(self.xl[:, s], self.ps[:, :, :], f32(self.xh[:, s]), ALU.subtract).then_inc(self.xl_done, 1)

    def pe_ready(self, pe, n):
        pe.wait_ge(self.xh_done, n + 1)
        pe.wait_ge(self.xl_done, n + 1)


def ffn_phase(nc, tag, X, ident, ps, W, small, jobs=(), hx=None):
    wh, wl = (part.rearrange("p (m k) c -> p m k c", k=KC) for part in W)
    gate_bias, in_c, bo_rows = small
    HALVES = T // GN
    UNITS = 8
    with Phase(nc) as ctx:
        sb = lambda n, s, d: ctx.enter_context(nc.sbuf_tensor(n, s, d))
        sem = lambda n: ctx.sem(n)
        norm = Norm(nc, sb, sem, ps[:, 0:2], ident, tag)
        gates = sb(f"{tag}_gates", [P, KC, 3, GN], F32)
        c = sb(f"{tag}_c", [P, HALVES, KC, GN], F32)
        ch = sb(f"{tag}_ch", [P, HALVES, KC, GN], F32R)
        cl = sb(f"{tag}_cl", [P, HALVES, KC, GN], F32R)
        hx = hx or sb(f"{tag}_hx", [P, TILES * C], F32)
        hc = sb(f"{tag}_hc", [P, HALVES, GW], F32)
        ring = ps[:, 2:2 + RING]
        unit_done = sem(f"{tag}_unit_done")
        unit_read = sem(f"{tag}_unit_read")
        ig_done = sem(f"{tag}_ig_done")
        fc_done = sem(f"{tag}_fc_done")
        c_done = sem(f"{tag}_c_done")
        ch_done = sem(f"{tag}_ch_done")
        c_split = sem(f"{tag}_c_split")
        hc_ready = sem(f"{tag}_hc_ready")
        hc_done = sem(f"{tag}_hc_done")
        sum_done = sem(f"{tag}_sum_done")
        tanh_done = sem(f"{tag}_tanh_done")
        x_done = sem(f"{tag}_x_done")
        split = SplitWeights(nc, sb, sem, tag, jobs)
        block = ctx.enter_context(nc.Block())

        def tile_of(i, h, j):
            return X[:, bass.ds(i * (HALVES * GW) + (h * GT + j) * C, C)]

        @block.tensor
        def _(pe):
            norm.pe_turn(pe, 0, 0)

            def step(i, last):
                for h in range(HALVES):
                    n = i * HALVES + h
                    norm.pe_ready(pe, n)
                    xh = lambda k: norm.xh[:, h, k, :]
                    xl = lambda k: norm.xl[:, h, k, :]
                    for u in range(2 * 3):
                        m, gate = u // 3, u % 3
                        pe.wait_ge(unit_read, n * UNITS + u + 1)
                        out = ring[:, u % RING]
                        w = lambda part, mat: lambda k: part[:, mat, k, m * P:(m + 1) * P]
                        matmul3(pe, out, w(wh, gate), w(wl, gate), xh, xl, range(KC), last=False)
                        pe.wait_ge(c_split, n + 1)
                        matmul3(pe, out, w(wh, 3 + gate), w(wl, 3 + gate), lambda k: ch[:, h, k, :],
                                lambda k: cl[:, h, k, :], range(KC), first=False).then_inc(unit_done, 1)
                        if u == 3 and not (last and h == HALVES - 1):
                            norm.pe_turn(pe, n + 1, (h + 1) % 2)
                    for u in range(6, UNITS):
                        pe.wait_ge(unit_read, n * UNITS + u + 1)
                        for t in range(2):
                            j = (u - 6) * 2 + t
                            ins = matmul3(pe, ring[:, u % RING, t * C:(t + 1) * C],
                                          lambda k: norm.xh[:, h, k, j * P:(j + 1) * P],
                                          lambda k: norm.xl[:, h, k, j * P:(j + 1) * P],
                                          lambda k: wh[:, 6, k, :], lambda k: wl[:, 6, k, :], range(KC))
                        ins.then_inc(unit_done, 1)

            with pe.Fori(0, B - 1) as i:
                step(i, False)
            step(B - 1, True)
            pe.wait_ge(c_split, (B + 1) * HALVES)
            pe.wait_ge(unit_read, RING + GROUPS * UNITS)
            for u in range(PT // 2):
                for t in range(2):
                    h, j = (2 * u + t) // GT, (2 * u + t) % GT
                    ins = matmul3(pe, ring[:, u, t * C:(t + 1) * C],
                                  lambda k: ch[:, h, k, j * P:(j + 1) * P],
                                  lambda k: cl[:, h, k, j * P:(j + 1) * P],
                                  lambda k: wh[:, 7, k, :], lambda k: wl[:, 7, k, :], range(KC))
                ins.then_inc(hc_ready, 1)

        @block.scalar
        def _(act):
            act.preload_act_table_set(SIGMOID_SET)
            act.sem_inc(unit_read, RING)
            norm.act_hi(act, 0, 0)

            def step(i, last):
                for h in range(HALVES):
                    n = i * HALVES + h
                    for u in range(2 * 3):
                        m, gate = u // 3, u % 3
                        if u == 0 or u == 3:
                            act.wait_ge(c_done, 2 * n + 1)
                        act.wait_ge(unit_done, n * UNITS + u + 1)
                        act.activation(gates[:, m, gate], ring[:, u % RING], ACT.Tanh if gate == 2 else ACT.Sigmoid,
                                       bias=gate_bias[:, gate * KC + m:gate * KC + m + 1]).then_inc(unit_read, 1)
                        if u == 4 and not (last and h == HALVES - 1):
                            norm.act_hi(act, n + 1, (h + 1) % 2)
                    for u in range(6, UNITS):
                        act.wait_ge(unit_done, n * UNITS + u + 1)
                        act.activation(hx[:, bass.ds(i * (HALVES * GW) + h * GW + (u - 6) * 2 * C, 2 * C)],
                                       ring[:, u % RING], ACT.Copy).then_inc(unit_read, 1)

            with act.Fori(0, B - 1) as i:
                step(i, False)
            step(B - 1, True)
            with act.Fori(0, B) as i:
                for h in range(HALVES):
                    act.wait_ge(sum_done, i * HALVES + h + 1)
                    cols = hx[:, bass.ds(i * (HALVES * GW) + h * GW, GW)]
                    act.activation(cols, cols, ACT.Tanh).then_inc(tanh_done, 1)

        @block.vector
        def _(dve):
            for h in range(HALVES):
                for k in range(KC):
                    ins = dve.tensor_copy(c[:, h, k], in_c[:, k:k + 1].broadcast_to([P, GN]))
            ins.then_inc(c_done, 1)
            dve.wait_ge(c_done, 1)
            dve.tensor_copy(ch[:, :, :, :], c[:, :, :, :]).then_inc(ch_done, 1)
            dve.wait_ge(ch_done, 1)
            dve.tensor_tensor(cl[:, :, :, :], c[:, :, :, :], f32(ch[:, :, :, :]), ALU.subtract).then_inc(c_split, 2)
            norm.dve_stats(dve, 0, 0, lambda j: tile_of(0, 0, j))
            norm.dve_apply(dve, 0, 0, lambda j: tile_of(0, 0, j))
            norm.dve_lo(dve, 0, 0)

            def update(n, h, m):
                f, g_in, g = (gates[:, m, q] for q in range(3))
                dve.wait_ge(unit_read, RING + n * UNITS + 3 * m + 3)
                dve.tensor_tensor(g_in, g_in, g, ALU.mult).then_inc(ig_done, 1)
                dve.tensor_tensor(f, f, c[:, h, m], ALU.mult).then_inc(fc_done, 1)
                dve.wait_ge(ig_done, 2 * n + m + 1)
                dve.wait_ge(fc_done, 2 * n + m + 1)
                dve.tensor_tensor(c[:, h, m], f, g_in, ALU.add).then_inc(c_done, 1)

            def step(i, last):
                for h in range(HALVES):
                    n = i * HALVES + h
                    more = not (last and h == HALVES - 1)
                    nxt = lambda j: tile_of(i + (h + 1) // 2, (h + 1) % 2, j)
                    if more:
                        norm.dve_stats(dve, n + 1, (h + 1) % 2, nxt)
                        norm.dve_apply(dve, n + 1, (h + 1) % 2, nxt)
                    update(n, h, 0)
                    if more:
                        norm.dve_lo(dve, n + 1, (h + 1) % 2)
                    update(n, h, 1)
                    dve.wait_ge(c_done, 2 * n + 3)
                    dve.wait_ge(unit_done, n * UNITS + 6)
                    dve.tensor_copy(ch[:, h], c[:, h]).then_inc(ch_done, 1)
                    dve.wait_ge(ch_done, n + 2)
                    dve.tensor_tensor(cl[:, h], c[:, h], f32(ch[:, h]), ALU.subtract).then_inc(c_split, 1)

            with dve.Fori(0, B - 1) as i:
                step(i, False)
            step(B - 1, True)
            for u in range(PT // 2):
                dve.wait_ge(hc_ready, u + 1)
                dve.tensor_tensor(hc[:, u // 2, (u % 2) * BANK:(u % 2 + 1) * BANK].rearrange("p (t c) -> p t c", t=2),
                                  ring[:, u].rearrange("p (t c) -> p t c", t=2),
                                  bo_rows[:, :].unsqueeze(1).broadcast_to([P, 2, C]), ALU.add).then_inc(hc_done, 1)
            dve.wait_ge(hc_done, PT // 2)
            dve.wait_ge(unit_read, RING + GROUPS * UNITS)

            def add(i, h):
                cols = hx[:, bass.ds(i * (HALVES * GW) + h * GW, GW)]
                dve.tensor_tensor(cols, cols, hc[:, h], ALU.add).then_inc(sum_done, 1)

            def residual(i, h):
                dve.wait_ge(tanh_done, i * HALVES + h + 1)
                cols = bass.ds(i * (HALVES * GW) + h * GW, GW)
                dve.scalar_tensor_tensor(out=X[:, cols], in0=hx[:, cols], scalar=0.5, in1=X[:, cols],
                                         op0=ALU.mult, op1=ALU.add).then_inc(x_done, 1)

            add(0, 0)
            with dve.Fori(0, B - 1) as i:
                add(i, 1)
                residual(i, 0)
                add(i + 1, 0)
                residual(i, 1)
            add(B - 1, 1)
            residual(B - 1, 0)
            residual(B - 1, 1)
            dve.wait_ge(x_done, GROUPS)

        @block.gpsimd
        def _(pool):
            norm.pool_setup(pool)
            for s in range(2):
                norm.pool_rstd(pool, s, s)
            with pool.Fori(1, GROUPS // 2) as i:
                for s in range(2):
                    norm.pool_rstd(pool, i * 2 + s, s)
            split.split(pool)

        @block.sync
        def _(sp):
            split.load(sp)


class SplitWeights:

    RAW = 2

    def __init__(self, nc, sb, sem, tag, jobs):
        part = lambda ap, a: ap[:, a:min(a + BANK, ap.shape[1])]
        self.jobs = [(part(src, a), part(hi, a), part(lo, a))
                     for src, hi, lo in jobs for a in range(0, src.shape[1], BANK)]
        self.raw = sb(f"{tag}_raw", [P, self.RAW, BANK], F32)
        self.loaded = [sem(f"{tag}_loaded{r}") for r in range(self.RAW)]
        self.hi_done = sem(f"{tag}_w_hi_done")
        self.lo_done = sem(f"{tag}_w_lo_done")

    def load(self, sp):
        for n, (src, _, _) in enumerate(self.jobs):
            if n >= self.RAW:
                sp.wait_ge(self.lo_done, n - self.RAW + 1)
            w = src.shape[1]
            sp.dma_start(self.raw[:, n % self.RAW, 0:w], src).then_inc(self.loaded[n % self.RAW], 16)

    def split(self, eng):
        for n, (src, hi, lo) in enumerate(self.jobs):
            w = src.shape[1]
            raw = self.raw[:, n % self.RAW, 0:w]
            eng.wait_ge(self.loaded[n % self.RAW], 16 * (n // self.RAW + 1))
            eng.tensor_copy(hi, raw).then_inc(self.hi_done, 1)
            eng.wait_ge(self.hi_done, n + 1)
            eng.tensor_tensor(lo, raw, f32(hi), ALU.subtract).then_inc(self.lo_done, 1)
        if self.jobs:
            eng.wait_ge(self.lo_done, len(self.jobs))


def load_phase(nc, X, x_dram, weights, smalls, masks):
    with Phase(nc) as ctx:
        sb = lambda n, s, d: ctx.enter_context(nc.sbuf_tensor(n, s, d))
        sem = lambda n: ctx.sem(n)
        split = SplitWeights(nc, sb, sem, "load", weights)
        mask_src, neg, ident16 = masks
        mask = sb("load_mask", [P, P], F32)
        small_in = sem("load_small_in")
        consts_done = sem("load_consts_done")
        x_in = sem("load_x_in")
        block = ctx.enter_context(nc.Block())

        @block.sync
        def _(sp):
            split.load(sp)

        @block.scalar
        def _(act):
            act.dma_start(mask[:, :], mask_src).then_inc(small_in, 16)
            for dst, src in smalls:
                act.dma_start(dst, src).then_inc(small_in, 16)
            xv = X[:, :].rearrange("p (t c) -> p t c", t=TILES)
            for b in range(B):
                act.dma_start(xv[:, b * PT:(b + 1) * PT], x_dram[b].rearrange("(t p) c -> p t c", p=P)).then_inc(x_in, 16)
            act.wait_ge(small_in, 16 * (len(smalls) + 1))
            act.wait_ge(x_in, 16 * B)

        @block.vector
        def _(dve):
            dve.wait_ge(small_in, 16 * (len(smalls) + 1))
            dve.tensor_copy(neg[:, :], mask[:, :]).then_inc(consts_done, 1)
            dve.tensor_copy(ident16[:, :], smalls[0][0]).then_inc(consts_done, 1)
            split.split(dve)
            dve.wait_ge(consts_done, 2)


def store_phase(nc, X, out):
    with Phase(nc) as ctx:
        stored = ctx.sem("x_stored")
        block = ctx.enter_context(nc.Block())

        @block.sync
        def _(sp):
            xv = X[:, :].rearrange("p (t c) -> p t c", t=TILES)
            for b in range(B):
                sp.dma_start(out[b].rearrange("(t p) c -> p t c", p=P), xv[:, b * PT:(b + 1) * PT]).then_inc(stored, 16)
            sp.wait_ge(stored, 16 * B)


def moe_phase(nc, tag, X, ident, ps, W, small, jobs=()):
    (eh, el), (gh, gl) = W
    gate_b, expert_b, iota = small
    CHUNKS = E * C // BANK
    with Phase(nc) as ctx:
        sb = lambda n, s, d: ctx.enter_context(nc.sbuf_tensor(f"{tag}_{n}", s, d))
        sem = lambda n: ctx.sem(f"{tag}_{n}")
        norm = Norm(nc, lambda n, s, d: ctx.enter_context(nc.sbuf_tensor(n, s, d)),
                    lambda n: ctx.sem(n), ps[:, 0:2], ident, tag)
        lg = sb("logits", [E, GN], F32)
        top = sb("top", [P, GT], F32)
        ex = sb("exp", [P, GT, E], F32)
        total = sb("total", [P, GT], F32)
        prob = sb("prob", [P, GT, E], F32)
        half = sb("half", [P, GT, E], F32)
        best = sb("best", [P, GT, 8], F32)
        place = sb("place", [P, GT, 8], U32)
        placef = sb("placef", [P, GT, 2], F32)
        pick = sb("pick", [P, 2, GT, E], F32)
        gsel = sb("gsel", [P, 2, GT, E], F32)
        gT = sb("gT", [E, 2, GN], F32)
        ring = ps[:, 2:2 + RING]
        logitsT = ps[0:E, 1, 0:GN]
        logits = ps[:, 0, 0:GT * E].rearrange("p (t e) -> p t e", t=GT)
        gselT = ps[0:E, 6, 0:GN]
        bias = ps[:, 7, 0:C]
        chunk_done = sem("chunk_done")
        lgT_done, lg_done, lt_done = sem("lgT_done"), sem("lg_done"), sem("lt_done")
        top_done, diff_done, exp_done = sem("top_done"), sem("diff_done"), sem("exp_done")
        total_done, rec_done, prob_done = sem("total_done"), sem("rec_done"), sem("prob_done")
        place_done, placef_done = sem("place_done"), sem("placef_done")
        pick_done, both_done, gsel_done = sem("pick_done"), sem("both_done"), sem("gsel_done")
        gT_turned, gT_done = sem("gT_turned"), sem("gT_done")
        bias_done, acc_step = sem("bias_done"), sem("acc_step")
        split = SplitWeights(nc, lambda n, s, d: ctx.enter_context(nc.sbuf_tensor(n, s, d)),
                             lambda n: ctx.sem(n), tag, jobs)
        block = ctx.enter_context(nc.Block())
        STEPS = GT * (E + 1)
        START = (E, 2 * E + 1, 3 * E + 2, 4 * E + 3)
        tile_of = lambda n, j: X[:, bass.ds(n * GW + j * C, C)]

        @block.tensor
        def _(pe):
            def logits_of(n, s):
                norm.pe_ready(pe, n)
                matmul3(pe, logitsT, lambda k: gh[:, k, :], lambda k: gl[:, k, :],
                        lambda k: norm.xh[:, s, k, :], lambda k: norm.xl[:, s, k, :], range(KC)).then_inc(lgT_done, 1)

            def turn_logits(n):
                for j in range(GT):
                    ins = pe.transpose(logits[:, j], lg[:, j * P:(j + 1) * P], ident[0:E, 0:E])
                ins.then_inc(lt_done, 1)

            def turn_gates(n, s):
                pe.wait_ge(gsel_done, n + 1)
                pe.wait_ge(gT_done, n)
                for j in range(GT):
                    ins = pe.transpose(gselT[:, j * P:(j + 1) * P], gsel[:, s, j], ident[:, :])
                ins.then_inc(gT_turned, 1)

            def experts(n, s, j, first=False, logits_next=None):
                for q in range(CHUNKS):
                    if q == CHUNKS - 1 and logits_next is not None:
                        pe.wait_ge(lg_done, logits_next + 1)
                    if j == 0:
                        pe.wait_ge(acc_step, n * STEPS + (START[3] - STEPS + 2 * q + 2))
                    else:
                        pe.wait_ge(acc_step, n * STEPS + (START[j - 1] + 2 * q + 2 + (first and j == 1)))
                    matmul3(pe, ring[:, q], lambda k: norm.xh[:, s, k, j * P:(j + 1) * P],
                            lambda k: norm.xl[:, s, k, j * P:(j + 1) * P],
                            lambda k: eh[:, k, q * BANK:(q + 1) * BANK],
                            lambda k: el[:, k, q * BANK:(q + 1) * BANK], range(KC)).then_inc(chunk_done, 1)

            def biases(n, s, j, added):
                if j == 0:
                    pe.wait_ge(gT_done, n + 1)
                pe.wait_ge(acc_step, added)
                pe.matmul(bias, gT[:, s, j * P:(j + 1) * P], expert_b[:, :],
                          start=True, stop=True).then_inc(bias_done, 1)

            def group(n, s, first=False, last=False):
                experts(n, s, 0)
                if not first:
                    biases(n - 1, 1 - s, 3, n * STEPS + E)
                turn_gates(n, s)
                if not last:
                    norm.pe_turn(pe, n + 1, 1 - s)
                experts(n, s, 1, first)
                biases(n, s, 0, n * STEPS + START[1])
                if not last:
                    logits_of(n + 1, 1 - s)
                experts(n, s, 2, logits_next=None if last else n + 1)
                biases(n, s, 1, n * STEPS + START[2])
                if not last:
                    turn_logits(n + 1)
                experts(n, s, 3)
                biases(n, s, 2, n * STEPS + START[3])
                if last:
                    biases(n, s, 3, n * STEPS + STEPS + E)

            norm.pe_turn(pe, 0, 0)
            logits_of(0, 0)
            pe.wait_ge(lg_done, 1)
            turn_logits(0)
            group(0, 0, first=True)
            with pe.Fori(0, GROUPS // 2 - 1) as i:
                group(i * 2 + 1, 1)
                group(i * 2 + 2, 0)
            group(GROUPS - 1, 1, last=True)


        @block.scalar
        def _(act):
            act.preload_act_table_set(EXP_SET)

            def prepare(n, s):
                norm.act_hi(act, n, s)
                act.wait_ge(lgT_done, n + 1)
                act.activation(lg[:, :], logitsT, ACT.Identity, bias=gate_b[:, 0:1]).then_inc(lg_done, 1)
                act.wait_ge(diff_done, n + 1)
                act.activation(ex[:, :, :], ex[:, :, :], ACT.Exp).then_inc(exp_done, 1)

            def gates(n, s):
                act.wait_ge(gT_turned, n + 1)
                act.activation(gT[:, s], gselT, ACT.Copy).then_inc(gT_done, 1)

            prepare(0, 0)
            with act.Fori(0, GROUPS // 2 - 1) as i:
                for s in range(2):
                    gates(i * 2 + s, s)
                    prepare(i * 2 + s + 1, 1 - s)
            gates(GROUPS - 2, 0)
            prepare(GROUPS - 1, 1)
            gates(GROUPS - 1, 1)

        @block.vector
        def _(dve):
            def softmax_in(n):
                dve.wait_ge(lt_done, n + 1)
                dve.tensor_reduce(top[:, :], logits, AX.X, ALU.max).then_inc(top_done, 1)
                dve.wait_ge(top_done, n + 1)
                dve.tensor_tensor(ex[:, :, :], logits, top[:, :].unsqueeze(2).broadcast_to([P, GT, E]),
                                  ALU.subtract).then_inc(diff_done, 1)

            def choose(n, s):
                dve.wait_ge(exp_done, n + 1)
                dve.tensor_reduce(total[:, :], ex[:, :, :], AX.X, ALU.add).then_inc(total_done, 1)
                dve.wait_ge(total_done, n + 1)
                dve.reciprocal(total[:, :], total[:, :]).then_inc(rec_done, 1)
                dve.wait_ge(rec_done, n + 1)
                dve.tensor_tensor(prob[:, :, :], ex[:, :, :], total[:, :].unsqueeze(2).broadcast_to([P, GT, E]),
                                  ALU.mult).then_inc(prob_done, 1)
                dve.wait_ge(prob_done, n + 1)
                dve.tensor_scalar(half[:, :, :], prob[:, :, :], 0.5, None, ALU.mult)
                for j in range(GT):
                    dve.max(best[:, j], prob[:, j])
                dve.drain()
                for j in range(GT):
                    ins = dve.max_index(place[:, j], best[:, j], prob[:, j])
                ins.then_inc(place_done, 1)
                dve.wait_ge(place_done, n + 1)
                dve.tensor_copy(placef[:, :, :], place[:, :, 0:2]).then_inc(placef_done, 1)
                dve.wait_ge(placef_done, n + 1)
                for r in range(2):
                    ins = dve.tensor_tensor(pick[:, r], iota[:, :].unsqueeze(1).broadcast_to([P, GT, E]),
                                            placef[:, :, r:r + 1].broadcast_to([P, GT, E]), ALU.is_equal)
                ins.then_inc(pick_done, 1)
                dve.wait_ge(pick_done, n + 1)
                dve.tensor_tensor(pick[:, 0], pick[:, 0], pick[:, 1], ALU.add).then_inc(both_done, 1)
                dve.wait_ge(both_done, n + 1)
                dve.tensor_tensor(gsel[:, s], half[:, :, :], pick[:, 0], ALU.mult).then_inc(gsel_done, 1)
                dve.wait_ge(gsel_done, n + 1)

            def experts(n, s, j, step):
                x = tile_of(n, j)
                for e in range(E):
                    if e % 2 == 0:
                        dve.wait_ge(chunk_done, (n * GT + j) * CHUNKS + e // 2 + 1)
                    if e:
                        dve.wait_ge(acc_step, step + e)
                    ins = dve.scalar_tensor_tensor(out=x, in0=ring[:, e // 2, (e % 2) * C:(e % 2 + 1) * C],
                                                   scalar=gsel[:, s, j, e:e + 1], in1=x, op0=ALU.mult, op1=ALU.add)
                    ins.then_inc(acc_step, 1)
                return step + E

            def biases(n, j, step):
                x = tile_of(n, j)
                dve.wait_ge(bias_done, n * GT + j + 1)
                dve.wait_ge(acc_step, step)
                dve.tensor_tensor(x, x, bias, ALU.add).then_inc(acc_step, 1)
                return step + 1

            def group(n, s, first=False, last=False):
                step = n * STEPS + (E + 1 if first else E)
                nxt = lambda j: tile_of(n + 1, j)
                if not last:
                    norm.dve_stats(dve, n + 1, 1 - s, nxt)
                    norm.dve_apply(dve, n + 1, 1 - s, nxt)
                step = experts(n, s, 0, step)
                if not first:
                    step = biases(n - 1, 3, step)
                if not last:
                    norm.dve_lo(dve, n + 1, 1 - s)
                step = experts(n, s, 1, step)
                step = biases(n, 0, step)
                step = experts(n, s, 2, step)
                step = biases(n, 1, step)
                if not last:
                    softmax_in(n + 1)
                step = experts(n, s, 3, step)
                step = biases(n, 2, step)
                if not last:
                    choose(n + 1, 1 - s)
                else:
                    biases(n, 3, step)

            dve.sem_inc(acc_step, E + 1)
            norm.dve_stats(dve, 0, 0, lambda j: tile_of(0, j))
            norm.dve_apply(dve, 0, 0, lambda j: tile_of(0, j))
            norm.dve_lo(dve, 0, 0)
            softmax_in(0)
            choose(0, 0)
            group(0, 0, first=True)
            with dve.Fori(0, GROUPS // 2 - 1) as i:
                group(i * 2 + 1, 1)
                group(i * 2 + 2, 0)
            group(GROUPS - 1, 1, last=True)
            dve.wait_ge(acc_step, E + GROUPS * STEPS + 1)

        @block.gpsimd
        def _(pool):
            norm.pool_setup(pool)
            for s in range(2):
                norm.pool_rstd(pool, s, s)
            with pool.Fori(1, GROUPS // 2) as i:
                for s in range(2):
                    norm.pool_rstd(pool, i * 2 + s, s)
            split.split(pool)

        @block.sync
        def _(sp):
            split.load(sp)


HEADS, HD = 16, C // 16
HG = 4
PARTS = 3
Q_PART = (0, 0, 0, 1, 1, 1, 2, 2)
K_PART = (0, 1, 2, 0, 1, 2, 0, 1)
COPIES = P // HD


def qkv_phase(nc, tag, X, ident, ps, W, V, parts_dram, proj_bias):
    wh, wl = W
    HALVES = T // GN
    QK = 2 * KC
    SCALE = (HD ** -0.5, HD ** -0.5, 1.0, 1.0)
    with Phase(nc) as ctx:
        sb = lambda n, s, d: ctx.enter_context(nc.sbuf_tensor(f"{tag}_{n}", s, d))
        sem = lambda n: ctx.sem(f"{tag}_{n}")
        norm = Norm(nc, lambda n, s, d: ctx.enter_context(nc.sbuf_tensor(n, s, d)),
                    lambda n: ctx.sem(n), ps[:, 0:2], ident, tag)
        part = sb("part", [P, HALVES, QK, PARTS, GN], BF16)
        rest = sb("rest", [P, 2, GN], F32)
        ring = ps[:, 2:2 + RING]
        unit_done, v_done, v_read = sem("unit_done"), sem("v_done"), sem("v_read")
        part0_done, part1_done, part2_done = sem("part0_done"), sem("part1_done"), sem("part2_done")
        rest_done, bias_added = sem("rest_done"), sem("bias_added")
        stored = [sem(f"stored{h}") for h in range(HALVES)]
        block = ctx.enter_context(nc.Block())
        tile_of = lambda i, h, j: X[:, bass.ds(i * (HALVES * GW) + (h * GT + j) * C, C)]

        @block.tensor
        def _(pe):
            norm.pe_turn(pe, 0, 0)

            def step(i, last):
                for h in range(HALVES):
                    n = i * HALVES + h
                    norm.pe_ready(pe, n)
                    for u in range(QK):
                        pe.wait_ge(rest_done, n * QK + u + 1)
                        w = lambda p: lambda k: p[:, k, u * P:(u + 1) * P]
                        matmul3(pe, ring[:, u], w(wh), w(wl), lambda k: norm.xh[:, h, k, :],
                                lambda k: norm.xl[:, h, k, :], range(KC)).then_inc(unit_done, 1)
                        if u == 1 and not (last and h == HALVES - 1):
                            norm.pe_turn(pe, n + 1, (h + 1) % 2)
                    for u in range(2):
                        pe.wait_ge(v_read, 2 * n + u + 1)
                        for t in range(2):
                            j = 2 * u + t
                            ins = matmul3(pe, ps[:, 6 + u, t * C:(t + 1) * C],
                                          lambda k: norm.xh[:, h, k, j * P:(j + 1) * P],
                                          lambda k: norm.xl[:, h, k, j * P:(j + 1) * P],
                                          lambda k: wh[:, k, 2 * C:3 * C], lambda k: wl[:, k, 2 * C:3 * C], range(KC))
                        ins.then_inc(v_done, 1)

            with pe.Fori(0, B - 1) as i:
                step(i, False)
            step(B - 1, True)

        @block.scalar
        def _(act):
            act.sem_inc(v_read, 2)
            norm.act_hi(act, 0, 0)

            def step(i, last):
                for h in range(HALVES):
                    n = i * HALVES + h
                    if not isinstance(i, int) or i:
                        act.wait_ge(stored[h], 16 * QK * i)
                    for u in range(QK):
                        act.wait_ge(unit_done, n * QK + u + 1)
                        act.activation(part[:, h, u, 0], ring[:, u], ACT.Copy, scale=SCALE[u]).then_inc(part0_done, 1)
                        if u == 3 and not (last and h == HALVES - 1):
                            norm.act_hi(act, n + 1, (h + 1) % 2)
                        if u:
                            second(n, h, u - 1)
                    second(n, h, QK - 1)
                    for u in range(2):
                        act.wait_ge(v_done, 2 * n + u + 1)
                        v = V[:, bass.ds(i * (PT * C), PT * C)].rearrange("p (g t d) -> p t g d", g=HEADS // HG, t=PT)
                        act.activation(v[:, h * GT + 2 * u:h * GT + 2 * u + 2], ps[:, 6 + u].rearrange(
                            "p (t g d) -> p t g d", t=2, g=HEADS // HG), ACT.Copy).then_inc(v_read, 1)

            def second(n, h, u):
                act.wait_ge(rest_done, RING + n * QK + u + 1)
                act.activation(part[:, h, u, 1], rest[:, u % 2], ACT.Copy).then_inc(part1_done, 1)

            with act.Fori(0, B - 1) as i:
                step(i, False)
            step(B - 1, True)

        @block.vector
        def _(dve):
            dve.sem_inc(rest_done, RING)
            norm.dve_stats(dve, 0, 0, lambda j: tile_of(0, 0, j))
            norm.dve_apply(dve, 0, 0, lambda j: tile_of(0, 0, j))
            norm.dve_lo(dve, 0, 0)

            def third(n, h, u):
                dve.wait_ge(part1_done, n * QK + u + 1)
                dve.tensor_tensor(part[:, h, u, 2], rest[:, u % 2], part[:, h, u, 1], ALU.subtract).then_inc(part2_done, 1)

            def step(i, last):
                for h in range(HALVES):
                    n = i * HALVES + h
                    more = not (last and h == HALVES - 1)
                    nxt = lambda j: tile_of(i + (h + 1) // 2, (h + 1) % 2, j)
                    if more:
                        norm.dve_stats(dve, n + 1, (h + 1) % 2, nxt)
                        norm.dve_apply(dve, n + 1, (h + 1) % 2, nxt)
                    for u in range(QK):
                        dve.wait_ge(part0_done, n * QK + u + 1)
                        dve.wait_ge(part2_done, n * QK + max(0, u - 1))
                        dve.scalar_tensor_tensor(out=rest[:, u % 2], in0=ring[:, u], scalar=SCALE[u],
                                                 in1=part[:, h, u, 0], op0=ALU.mult, op1=ALU.subtract).then_inc(rest_done, 1)
                        if u:
                            third(n, h, u - 1)
                        if u == 3 and more:
                            norm.dve_lo(dve, n + 1, (h + 1) % 2)
                    third(n, h, QK - 1)

            with dve.Fori(0, B - 1) as i:
                step(i, False)
            step(B - 1, True)

        @block.gpsimd
        def _(pool):
            norm.pool_setup(pool)
            rows = proj_bias[:, :].unsqueeze(1).broadcast_to([P, GT, C])

            def bias(n, col):
                pool.wait_ge(norm.xn_done, n + 1)
                x = X[:, bass.ds(col, GW)].rearrange("p (t c) -> p t c", t=GT)
                pool.tensor_tensor(x, x, rows, ALU.add).then_inc(bias_added, 1)

            norm.pool_rstd(pool, 0, 0)
            norm.pool_rstd(pool, 1, 1)
            bias(0, 0)
            with pool.Fori(0, GROUPS // 2 - 1) as i:
                norm.pool_rstd(pool, i * 2 + 2, 0)
                bias(i * 2 + 1, i * (2 * GW) + GW)
                norm.pool_rstd(pool, i * 2 + 3, 1)
                bias(i * 2 + 2, i * (2 * GW) + 2 * GW)
            bias(GROUPS - 1, (GROUPS - 1) * GW)
            pool.wait_ge(bias_added, GROUPS)

        @block.sync
        def _(sp):
            with sp.Fori(0, B) as i:
                for h in range(HALVES):
                    for u in range(QK):
                        sp.wait_ge(part2_done, (i * HALVES + h) * QK + u + 1)
                        rows = bass.ds(i * C + u % KC * P, P)
                        dst = parts_dram[u // KC, :, rows, h * GN:(h + 1) * GN].rearrange("a r t -> r a t")
                        sp.dma_start(dst, part[:, h, u]).then_inc(stored[h], 16)
            for h in range(HALVES):
                sp.wait_ge(stored[h], 16 * QK * B)


def attention_phase(nc, tag, ident, ps, V, parts_dram, neg, ident16):
    BLOCKS = T // BANK
    pass_units, pass_steps = [], []
    for qb in range(BLOCKS):
        first = qb * GT
        tiles = [[(kj, 0, 0)] for kj in range(first + 1)]
        tiles += [[(first + 1, 0, P), (first + 3, 3 * P, 3 * P)]]
        for together in tiles:
            at = len(pass_units)
            for pair in range(2):
                pass_units.append([(2 * pair + t, kj, t, c, q0) for t in range(2) for kj, c, q0 in together])
            pass_steps.append((qb, at + 1, [(h, kj, at + h // 2, h % 2, c, q0) for kj, c, q0 in together for h in range(HG)]))
        at = len(pass_units)
        pass_units.append([(h, first + 2, h // 2, h % 2 * 2 * P, 2 * P) for h in range(HG)])
        pass_steps.append((qb, at, [(h, first + 2, at, h // 2, h % 2 * 2 * P, 2 * P) for h in range(HG)]))
    PU, PS = len(pass_units), len(pass_steps)
    NU, NS = 2 * PU, 2 * PS
    BODIES = B * HEADS // HG // 2
    step_end = [s * PU + pass_steps[m][1] for s in range(2) for m in range(PS)]
    step_of = [min(m for m in range(NS) if step_end[m] >= u) for u in range(NU)]
    BLOCK_STEPS = [m for m in range(NS) if m % PS == PS - 1 or pass_steps[m % PS + 1][0] != pass_steps[m % PS][0]]
    BLOCK_UNITS = [step_end[m] for m in BLOCK_STEPS]
    AHEAD = 6
    TURN_LAG, COPY_LAG, OUT_LAG = 2, 7, 9
    SU, WU = 3, 12
    assert NU % SU == 0 and NU % WU == 0
    DVE_SQUARES = 6
    LIMIT = 2.0 ** 60

    def outputs_at(x, ends, n, lag, i, first, stage):
        for k, end in enumerate(ends):
            back, at = divmod(end + lag, n)
            if at == x and not (first and back):
                stage((i - back) * len(ends) + k, i - back, k)

    def outputs_left(ends, n, lag, i, stage):
        for k, end in enumerate(ends):
            if end + lag >= n:
                stage(i * len(ends) + k, i, k)

    by_dve = lambda u: u % DVE_SQUARES == DVE_SQUARES - 1
    dve_count = [sum(by_dve(x) for x in range(u)) for u in range(NU + 1)]
    with Phase(nc) as ctx:
        sb = lambda n, s, d: ctx.enter_context(nc.sbuf_tensor(f"{tag}_{n}", s, d))
        sem = lambda n: ctx.sem(f"{tag}_{n}")
        SQ = sb("q_stack", [P, 2, HG, T], BF16)
        SK = sb("k_stack", [P, 2, HG, T], BF16)
        va = sb("v_ones", [P, 2, PT, HG, 2 * HD], F32)
        Wt = sb("weights", [P, WU, 2, BANK], F32)
        oT = sb("oT", [P, 2, BANK], F32)
        den = sb("den", [P, GT, HG], F32)
        scores = lambda u: ps[:, 2 * (u % SU):2 * (u % SU) + 2]
        O = lambda k: ps[:, 6 + k % 2]
        loaded = [sem(f"loaded{s}") for s in range(2)]
        ones_set, v_copied = sem("ones_set"), sem("v_copied")
        s_done, exp_done, clamp_done, ln_done, max_done = (sem(n) for n in ("s_done", "exp_done", "clamp_done", "ln_done", "max_done"))
        sq_pool, sq_dve, pv_done = sem("sq_pool"), sem("sq_dve"), sem("pv_done")
        oT_done, o_turned, den_done, rec_done, o_done = (sem(n) for n in ("oT_done", "o_turned", "den_done", "rec_done", "o_done"))
        block = ctx.enter_context(nc.Block())

        @block.tensor
        def _(pe):
            def score_unit(i, u):
                i, u = i + u // NU, u % NU
                s, segments = u // PU, pass_units[u % PU]
                if u % PU == 0:
                    pe.wait_ge(loaded[s], (i + 1) * (16 * 2 * COPIES))
                pe.wait_ge(max_done, i * NU + u + 1)
                for h, kj, t, c, q0 in segments:
                    diagonal = kj // GT == u_block(u)
                    q = u_block(u) * BANK + q0
                    w = segment_width(kj, u_block(u))
                    ins = pe.matmul(scores(u)[:, t, c:c + w], SK[:, s, h, kj * P:(kj + 1) * P],
                                    SQ[:, s, h, q:q + w], start=True, stop=not diagonal)
                    if diagonal:
                        ins = pe.matmul(scores(u)[:, t, c:c + P], neg[:, :], ident16[:, :], start=False, stop=True)
                ins.then_inc(s_done, 1)

            def value_step(i, m):
                s, (qb, _, products), u = m // PS, pass_steps[m % PS], step_end[m]
                if m % PS == 0:
                    pe.wait_ge(v_copied, 2 * i + s + 1)
                if products[0][1] == 0:
                    pe.wait_ge(o_done, (i * 2 + s) * BLOCKS + qb + 1)
                pe.wait_ge(sq_pool, i * (NU - dve_count[NU]) + (u + 1 - dve_count[u + 1]))
                pe.wait_ge(sq_dve, i * dve_count[NU] + dve_count[u + 1])
                for h, kj, unit, t, c, q0 in products:
                    w = segment_width(kj, qb)
                    ins = pe.matmul(O(qb)[h * 2 * HD:(h + 1) * 2 * HD, q0:q0 + w], va[:, s, kj, h],
                                    Wt[:, (s * PU + unit) % WU, t, c:c + w], start=kj == 0, stop=m in BLOCK_STEPS)
                ins.then_inc(pv_done, 1)

            def turn_output(n, i, k):
                pe.wait_ge(oT_done, n + 1)
                for j in range(GT):
                    ins = pe.transpose(O(k)[:, j * P:(j + 1) * P], oT[:, k % 2, j * P:(j + 1) * P], ident[:, :])
                ins.then_inc(o_turned, 1)

            def body(i, first=False, last=False):
                for m in range(NS):
                    for u in range(step_end[m - 1] + 1 if m else 0, step_end[m] + 1):
                        if not (last and u + AHEAD >= NU):
                            score_unit(i, u + AHEAD)
                    value_step(i, m)
                    outputs_at(m, BLOCK_STEPS, NS, TURN_LAG, i, first, turn_output)
                if last:
                    outputs_left(BLOCK_STEPS, NS, TURN_LAG, i, turn_output)

            u_block = lambda u: [qb for qb, end, _ in pass_steps if end >= u % PU][0]
            segment_width = lambda kj, qb: BANK - max(0, kj * P - qb * BANK)
            for u in range(AHEAD):
                score_unit(0, u)
            body(0, first=True)
            with pe.Fori(1, BODIES - 1) as i:
                body(i)
            body(BODIES - 1, last=True)

        @block.scalar
        def _(act):
            act.preload_act_table_set(LN_EXP_SET)

            def exp(i, u):
                i, u = i + u // NU, u % NU
                act.wait_ge(s_done, i * NU + u + 1)
                before = step_of[u - WU] + NS if u >= WU else step_of[u - WU + NU]
                act.wait_ge(pv_done, i * NS + before + 1)
                act.activation(Wt[:, u % WU], scores(u), ACT.Exp).then_inc(exp_done, 1)

            def ln(i, u):
                act.wait_ge(clamp_done, i * NU + u + 1)
                act.activation(Wt[:, u % WU], Wt[:, u % WU], ACT.Ln, bias=1.0).then_inc(ln_done, 1)

            def copy_output(n, i, k):
                act.wait_ge(pv_done, (i + 1) * NS + BLOCK_STEPS[k] + 1)
                act.wait_ge(o_turned, n + 1)
                act.activation(oT[:, k % 2], O(k), ACT.Copy).then_inc(oT_done, 1)

            def body(i, first=False, last=False):
                for u in range(NU):
                    if not (last and u == NU - 1):
                        exp(i, u + 1)
                    ln(i, u)
                    outputs_at(u, BLOCK_UNITS, NU, COPY_LAG, i, first, copy_output)
                if last:
                    outputs_left(BLOCK_UNITS, NU, COPY_LAG, i, copy_output)

            act.sem_inc(o_turned, 2)
            act.sem_inc(o_done, 2)
            act.sem_inc(pv_done, NS)
            exp(0, 0)
            body(0, first=True)
            with act.Fori(1, BODIES - 1) as i:
                body(i)
            body(BODIES - 1, last=True)

        @block.vector
        def _(dve):
            def clamp(i, u):
                i, u = i + u // NU, u % NU
                dve.wait_ge(exp_done, i * NU + u + 1)
                dve.tensor_scalar(Wt[:, u % WU], Wt[:, u % WU], LIMIT, None, ALU.min).then_inc(clamp_done, 1)

            def softplus(i, u):
                wt = Wt[:, u % WU]
                dve.wait_ge(ln_done, i * NU + u + 1)
                dve.tensor_tensor(wt, scores(u), wt, ALU.max).then_inc(max_done, 1)
                if by_dve(u):
                    dve.wait_ge(max_done, SU + i * NU + u + 1)
                    dve.tensor_tensor(wt, wt, wt, ALU.mult).then_inc(sq_dve, 1)

            def divide_output(n, i, k):
                cells = O(k).rearrange("p (j h d) -> p j h d", j=GT, h=HG)
                dve.wait_ge(o_turned, 2 + n + 1)
                dve.tensor_scalar(den[:, :, :], cells[:, :, :, HD], 1e-9, None, ALU.add).then_inc(den_done, 1)
                dve.wait_ge(den_done, n + 1)
                dve.reciprocal(den[:, :, :], den[:, :, :]).then_inc(rec_done, 1)
                dve.wait_ge(rec_done, n + 1)
                out = V[:, bass.ds((i * 2 + k // BLOCKS) * (PT * HG * HD) + k % BLOCKS * (GT * HG * HD), GT * HG * HD)]
                dve.tensor_tensor(out.rearrange("p (j h d) -> p j h d", j=GT, h=HG), cells[:, :, :, 0:HD],
                                  den[:, :, :].unsqueeze(3).broadcast_to([P, GT, HG, HD]), ALU.mult).then_inc(o_done, 1)

            def body(i, first=False, last=False):
                for u in range(NU):
                    if not (last and u == NU - 1):
                        clamp(i, u + 1)
                    softplus(i, u)
                    outputs_at(u, BLOCK_UNITS, NU, OUT_LAG, i, first, divide_output)
                if last:
                    outputs_left(BLOCK_UNITS, NU, OUT_LAG, i, divide_output)

            dve.sem_inc(max_done, SU)
            clamp(0, 0)
            body(0, first=True)
            with dve.Fori(1, BODIES - 1) as i:
                body(i)
            body(BODIES - 1, last=True)

        @block.gpsimd
        def _(pool):
            pool.memset(va[:, :, :, :, :], 1.0).then_inc(ones_set, 1)
            pool.wait_ge(ones_set, 1)

            def copy_v(i, s, used):
                pool.wait_ge(pv_done, used)
                v = V[:, bass.ds((i * 2 + s) * (PT * HG * HD), PT * HG * HD)]
                pool.tensor_copy(va[:, s, :, :, 0:HD], v.rearrange("p (t h d) -> p t h d", t=PT, h=HG)).then_inc(v_copied, 1)

            def body(i, last=False):
                for u in range(NU):
                    if not by_dve(u):
                        pool.wait_ge(max_done, SU + i * NU + u + 1)
                        pool.tensor_tensor(Wt[:, u % WU], Wt[:, u % WU], Wt[:, u % WU], ALU.mult).then_inc(sq_pool, 1)
                    if u == NU // 3:
                        copy_v(i, 1, (i + 1) * NS)
                    if u == NU * 5 // 6 and not last:
                        copy_v(i + 1, 0, (i + 1) * NS + PS)

            copy_v(0, 0, 0)
            with pool.Fori(0, BODIES - 1) as i:
                body(i)
            body(BODIES - 1, last=True)

        @block.sync
        def _(sp):
            def load(i, s):
                for stack, q_or_k, parts in ((SQ, 0, Q_PART), (SK, 1, K_PART)):
                    for n, part in enumerate(parts):
                        src = parts_dram[q_or_k, part, bass.ds((i * 2 + s) * (HG * HD), HG * HD), :]
                        sp.dma_start(stack[n * HD:(n + 1) * HD, s],
                                     src.rearrange("(h d) t -> d h t", h=HG)).then_inc(loaded[s], 16)

            load(0, 0)
            load(0, 1)
            with sp.Fori(1, BODIES) as i:
                for s in range(2):
                    sp.wait_ge(s_done, i * NU + (s - 1) * (NU // 2))
                    load(i, s)


def projection_phase(nc, tag, X, ident, ps, W, V):
    wh, wl = W
    with Phase(nc) as ctx:
        sb = lambda n, s, d: ctx.enter_context(nc.sbuf_tensor(f"{tag}_{n}", s, d))
        sem = lambda n: ctx.sem(f"{tag}_{n}")
        o = sb("o", [P, 2, GT, C], F32)
        oh = sb("oh", [P, 2, KC, GN], F32R)
        ol = sb("ol", [P, 2, KC, GN], F32R)
        turn = ps[:, 0:2]
        o_in, turned, oh_done, ol_done = sem("o_in"), sem("turned"), sem("oh_done"), sem("ol_done")
        y_done, x_done = sem("y_done"), sem("x_done")
        block = ctx.enter_context(nc.Block())
        HALVES = T // GN

        @block.scalar
        def _(act):
            def copy_in(i, h):
                n = i * HALVES + h
                if not isinstance(i, int) or i:
                    act.wait_ge(turned, n - 1)
                v = V[:, bass.ds(i * (PT * C), PT * C)].rearrange("p (g t d) -> p t g d", g=HEADS // HG, t=PT)
                act.activation(o[:, h].rearrange("p t (g d) -> p t g d", g=HEADS // HG),
                               v[:, h * GT:(h + 1) * GT], ACT.Copy).then_inc(o_in, 1)

            def hi(n, h):
                act.wait_ge(turned, n + 1)
                act.activation(oh[:, h], turn, ACT.Copy).then_inc(oh_done, 1)

            copy_in(0, 0)
            copy_in(0, 1)
            with act.Fori(0, B - 1) as i:
                for h in range(HALVES):
                    hi(i * HALVES + h, h)
                    copy_in(i + 1, h)
            for h in range(HALVES):
                hi((B - 1) * HALVES + h, h)

        @block.tensor
        def _(pe):
            def turn_in(n, s):
                pe.wait_ge(o_in, n + 1)
                pe.wait_ge(ol_done, n)
                for k in range(KC):
                    for j in range(GT):
                        ins = pe.transpose(turn[:, k, j * P:(j + 1) * P], o[:, s, j, k * P:(k + 1) * P], ident[:, :])
                ins.then_inc(turned, 1)

            def project(n, s):
                pe.wait_ge(ol_done, n + 1)
                for u in range(2):
                    pe.wait_ge(x_done, 2 * n + u + 1)
                    for t in range(2):
                        j = 2 * u + t
                        ins = matmul3(pe, ps[:, 2 + 2 * s + u, t * C:(t + 1) * C],
                                      lambda k: oh[:, s, k, j * P:(j + 1) * P], lambda k: ol[:, s, k, j * P:(j + 1) * P],
                                      lambda k: wh[:, k, :], lambda k: wl[:, k, :], range(KC))
                    ins.then_inc(y_done, 1)

            turn_in(0, 0)
            with pe.Fori(0, GROUPS // 2 - 1) as i:
                turn_in(i * 2 + 1, 1)
                project(i * 2, 0)
                turn_in(i * 2 + 2, 0)
                project(i * 2 + 1, 1)
            turn_in(GROUPS - 1, 1)
            project(GROUPS - 2, 0)
            project(GROUPS - 1, 1)

        @block.vector
        def _(dve):
            dve.sem_inc(x_done, 4)

            def lo(n, s):
                dve.wait_ge(oh_done, n + 1)
                dve.tensor_tensor(ol[:, s], turn, f32(oh[:, s]), ALU.subtract).then_inc(ol_done, 1)

            def residual(n, s):
                for u in range(2):
                    x = X[:, bass.ds(n * GW + u * 2 * C, 2 * C)]
                    dve.wait_ge(y_done, 2 * n + u + 1)
                    dve.tensor_tensor(x, x, ps[:, 2 + 2 * s + u], ALU.add).then_inc(x_done, 1)

            lo(0, 0)
            with dve.Fori(0, GROUPS // 2 - 1) as i:
                lo(i * 2 + 1, 1)
                residual(i * 2, 0)
                lo(i * 2 + 2, 0)
                residual(i * 2 + 1, 1)
            lo(GROUPS - 1, 1)
            residual(GROUPS - 2, 0)
            residual(GROUPS - 1, 1)
            dve.wait_ge(x_done, 4 + 2 * GROUPS)


DI, NH, DH, DS = 2 * C, 8, 64, P
FT = DI // P
TAPS = 4
RMS_EPS = 1e-6
PROJ = 2 * DI + 2 * DS + NH


def ssm_phase(nc, tag, X, ident, ps, W_in, W_out, spare, consts, decay_dram):
    wh, wl = W_in
    oh, ol = W_out
    c_dram = consts
    with Phase(nc) as ctx:
        sb_ = lambda n, s, d: ctx.enter_context(nc.sbuf_tensor(n, s, d))
        sem_ = lambda n: ctx.sem(n)
        sb = lambda n, s, d=F32: sb_(f"{tag}_{n}", s, d)
        sem = lambda n: sem_(f"{tag}_{n}")
        norm = Norm(nc, sb_, sem_, ps[:, 0:2], ident, tag, slots=1)
        tri = sb("tri", [P, P])
        conv_w, conv_b, d_col = sb("conv_w", [P, FT, TAPS]), sb("conv_b", [P, FT]), sb("d_col", [P, FT])
        norm_w, dt_bias, neg_a = sb("norm_w", [P, C]), sb("dt_bias", [P, NH]), sb("neg_a", [P, NH])
        mv2, ms, r2 = sb("mv2", [P, GT, 2]), sb("ms", [P, GT]), sb("r2", [P, GT])
        xpad = sb("xpad", [P, FT, GT, TAPS - 1 + P])
        xc = sb("xc", [P, 2, FT, GT, P])
        zs = sb("zs", [P, FT, GT, P])
        bT, cT = sb("bT", [P, GT, P]), sb("cT", [P, 2, GT, P])
        b_tm = sb("b_tm", [P, GT, P])
        cb = sb("cb", [P, 2, GT, P])
        dtT = sb("dtT", [NH, GN])
        dt0, dta, dt = sb("dt0", [P, GT, NH]), sb("dta", [P, GT, NH]), sb("dt", [P, 2, GT, NH])
        a = sb("a", [P, GT, NH])
        l_tok = sb("l_tok", [P, 2, GT, NH])
        l_row = sb("l_row", [GT * NH, P])
        lb = sb("lb", [P, 2, NH, P])
        e0 = sb("e0", [P, NH, P])
        dec = sb("dec", [P, 2, NH, P])
        cts = sb("cts", [P, 2, NH, P])
        edge = sb("edge", [P, 2, 2, NH])
        xdt = sb("xdt", [P, 2, NH, DH])
        xd2 = sb("xd2", [P, NH, DH])
        H = sb("H", [P, GT, NH, DH])
        y = sb("y", [P, FT, P])
        yh, yl = spare

        small = ps[:, 4, :]
        ps_dt = small[:, 0:GT * NH].rearrange("p (b h) -> p b h", b=GT)
        ps_lrow = small[0:GT * NH, P:2 * P]
        ps_b = small.rearrange("p (b n) -> p b n", b=GT)
        ps_cb = ps[:, 5].rearrange("p (b n) -> p b n", b=GT)
        ps_x, ps_y, ps_h, ps_o = ps[:, 5], ps[:, 6], ps[:, 7], ps[:, 7, 0:C]

        (const_in, ln_done, mv2_done, sq_done, msum_done, ms_done, r2_done, add_done,
         init_done) = (sem(n) for n in ("const_in", "ln_done", "mv2_done", "sq_done", "msum_done",
                                        "ms_done", "r2_done", "add_done", "init_done"))
        (unit_done, unit_read, conv_step, halo_done, xc_done, dt_turned, dt0_done, dta_done, dte_done, dtl_done,
         dt_done, a_done, l_done, l_copied, l_stored, b_turned, b_copied, cb_done, cbm_done) = (
            sem(n) for n in ("unit_done", "unit_read", "conv_step", "halo_done", "xc_done", "dt_turned", "dt0_done",
                             "dta_done", "dte_done", "dtl_done", "dt_done", "a_done", "l_done", "l_copied",
                             "l_stored", "b_turned", "b_copied", "cb_done", "cbm_done"))
        lb_in = [sem(f"lb_in{r}") for r in range(2)]
        (dsub_done, edge_in, dexp_done, edge_done, e0_done, w_done, cts_done, x_turned, xdt_done, xd2_done, y_summed,
         yd_done, y_done, yh_done, yl_done, state_done, h_decayed, h_done, out_done, x_done) = (
            sem(n) for n in ("dsub_done", "edge_in", "dexp_done", "edge_done", "e0_done", "w_done", "cts_done",
                             "x_turned", "xdt_done", "xd2_done", "y_summed", "yd_done", "y_done", "yh_done", "yl_done",
                             "state_done", "h_decayed", "h_done", "out_done", "x_done"))
        block = ctx.enter_context(nc.Block())

        U_DT, U_B, U_C, U_X, U_Z = 0, 1, 2, 3, 3 + FT
        UNITS = 3 + 2 * FT
        COLS = {U_DT: (2 * DI + 2 * DS, NH), U_B: (2 * DI, DS), U_C: (2 * DI + DS, DS)}
        COLS.update({U_X + f: (DI + f * P, P) for f in range(FT)})
        COLS.update({U_Z + f: (f * P, P) for f in range(FT)})
        unit_bank = lambda v, u: ps[:, 2 + (v + u) % 2]
        tile_of = lambda p, b: X[:, bass.ds(p * C + b * (PT * C), C)]

        def groups(eng, group):
            with eng.Fori(0, PT // 2 - 1) as i:
                group(i * 2, 0, False)
                group(i * 2 + 1, 1, False)
            group(PT - 2, 0, False)
            group(PT - 1, 1, True)

        @block.tensor
        def _(pe):
            def unit(p, v, u):
                at, m = COLS[u]
                pe.wait_ge(unit_read, p * UNITS + u + 1)
                matmul3(pe, unit_bank(v, u)[0:m], lambda k: wh[:, k, at:at + m], lambda k: wl[:, k, at:at + m],
                        lambda k: norm.xh[:, 0, k, :], lambda k: norm.xl[:, 0, k, :], range(KC)).then_inc(unit_done, 1)

            def piece(p, v, b):
                if b == 0:
                    norm.pe_turn(pe, p, 0)
                    norm.pe_ready(pe, p)
                    unit(p, v, U_DT)
                if b == 1:
                    unit(p, v, U_B)
                    unit(p, v, U_C)
                    pe.wait_ge(unit_read, 2 + p * UNITS + U_DT + 1)
                    pe.wait_ge(b_copied, p)
                    unit(p, v, U_X)
                    for t in range(GT):
                        ins = pe.transpose(ps_dt[:, t], dtT[:, t * P:(t + 1) * P], ident[0:NH, 0:NH])
                    ins.then_inc(dt_turned, 1)
                    unit(p, v, U_X + 1)
                if b == 2:
                    unit(p, v, U_X + 2)
                    pe.wait_ge(a_done, p + 1)
                    pe.matmul(ps_dt, tri[:, :], a[:, :, :], start=True, stop=True)
                    pe.matmul(ps_lrow, a[:, :, :].rearrange("p b h -> p (b h)"), tri[:, :], start=True, stop=True)\
                        .then_inc(l_done, 1)
                    unit(p, v, U_X + 3)
                if b == 3:
                    pe.wait_ge(l_copied, 2 * (p + 1))
                    for t in range(GT):
                        ins = pe.transpose(ps_b[:, t], bT[:, t], ident[:, :])
                    ins.then_inc(b_turned, 1)
                    pe.wait_ge(xdt_done, p * GT)
                    for t in range(GT):
                        ins = pe.matmul(ps_cb[:, t], bT[:, t], cT[:, v, t], start=True, stop=True)
                    ins.then_inc(cb_done, 1)

            def turn_x(p, v, b):
                pe.wait_ge(xc_done, p + 1)
                pe.wait_ge(xdt_done, p * GT + b)
                if b == 0:
                    pe.wait_ge(cbm_done, p + 1)
                for f in range(FT):
                    ins = pe.transpose(ps_x[:, f * P:(f + 1) * P], xc[:, v, f, b], ident[:, :])
                ins.then_inc(x_turned, 1)

            def tile_y(p, v, b):
                n = p * GT + b
                pe.wait_ge(w_done, n + 1)
                pe.wait_ge(cts_done, n + 1)
                pe.wait_ge(h_done, n + 1)
                pe.wait_ge(y_done, n)
                for h in range(NH):
                    out = ps_y[h % 2 * DH:(h % 2 + 1) * DH, h // 2 * P:(h // 2 + 1) * P]
                    pe.matmul(out, xdt[:, b % 2, h], dec[:, b % 2, h], start=True, stop=False)
                    ins = pe.matmul(out, H[:, b, h], cts[:, b % 2, h], start=False, stop=True)
                ins.then_inc(y_summed, 1)

            def tile_state(p, v, b):
                n = p * GT + b
                pe.wait_ge(xd2_done, n + 1)
                pe.wait_ge(x_done, n)
                pe.matmul(ps_h, b_tm[:, b], xd2[:, :, :].rearrange("p h d -> p (h d)"), start=True, stop=True)\
                    .then_inc(state_done, 1)

            def tile_out(p, v, b):
                n = p * GT + b
                pe.wait_ge(yl_done, n + 1)
                pe.wait_ge(h_done, GT + n + 1)
                matmul3(pe, ps_o, lambda k: yh[:, k], lambda k: yl[:, k], lambda k: oh[:, k], lambda k: ol[:, k],
                        range(FT)).then_inc(out_done, 1)

            def group(p, v, last):
                turn_x(p, v, 0)
                for f in range(FT):
                    unit(p, v, U_Z + f)
                for b in range(GT):
                    if b + 1 < GT:
                        turn_x(p, v, b + 1)
                    tile_y(p, v, b)
                    tile_state(p, v, b)
                    if not last and b < 3:
                        piece(p + 1, 1 - v, b)
                    tile_out(p, v, b)
                if not last:
                    piece(p + 1, 1 - v, 3)

            pe.wait_ge(init_done, 4)
            for b in range(GT):
                piece(0, 0, b)
            groups(pe, group)

        @block.scalar
        def _(act):
            def unit(p, v, u, func=ACT.Copy):
                act.wait_ge(unit_done, p * UNITS + u + 1)
                bank = unit_bank(v, u)
                as_tiles = lambda ap: ap.rearrange("p (b t) -> p b t", b=GT)
                if u == U_DT:
                    out, src = dtT[:, :], bank[0:NH]
                elif u == U_B:
                    out, src = bT[:, :, :], as_tiles(bank)
                elif u == U_C:
                    out, src = cT[:, v], as_tiles(bank)
                elif u < U_Z:
                    act.wait_ge(halo_done, p * FT + (u - U_X) + 1)
                    out, src = xpad[:, u - U_X, :, TAPS - 1:], as_tiles(bank)
                else:
                    out, src = zs[:, u - U_Z], as_tiles(bank)
                act.activation(out, src, func).then_inc(unit_read, 1)

            def piece(p, v, b):
                if b == 0:
                    norm.act_hi(act, p, 0)
                    unit(p, v, U_DT)
                if b == 1:
                    unit(p, v, U_B)
                    unit(p, v, U_C)
                    unit(p, v, U_X)
                    unit(p, v, U_X + 1)
                    act.wait_ge(dta_done, p + 1)
                    act.activation(dta[:, :, :], dta[:, :, :], ACT.Exp, scale=-1.0).then_inc(dte_done, 1)
                    act.wait_ge(dte_done, p + 1)
                    act.activation(dta[:, :, :], dta[:, :, :], ACT.Ln, bias=1.0).then_inc(dtl_done, 1)
                if b == 2:
                    unit(p, v, U_X + 2)
                    act.wait_ge(l_done, p + 1)
                    act.wait_ge(l_stored, 16 * p)
                    act.activation(l_row[:, :], ps_lrow, ACT.Copy).then_inc(l_copied, 1)
                    act.activation(l_tok[:, v], ps_dt, ACT.Copy).then_inc(l_copied, 1)
                    unit(p, v, U_X + 3)
                if b == 3:
                    act.wait_ge(b_turned, p + 1)
                    act.wait_ge(state_done, p * GT)
                    act.activation(b_tm[:, :, :], ps_b, ACT.Copy).then_inc(b_copied, 1)

            def decays(n, b):
                r = b % 2
                act.wait_ge(dsub_done, n + 1)
                act.activation(dec[:, r], dec[:, r], ACT.Exp).then_inc(dexp_done, 1)
                act.wait_ge(edge_in, n + 1)
                act.activation(edge[:, r], edge[:, r], ACT.Exp).then_inc(edge_done, 1)
                act.wait_ge(cts_done, n)
                act.activation(e0[:, :, :], lb[:, r], ACT.Exp).then_inc(e0_done, 1)

            def group(p, v, last):
                act.wait_ge(conv_step, (p + 1) * FT * TAPS)
                act.activation(xc[:, v], xc[:, v], ACT.Silu).then_inc(xc_done, 1)
                act.wait_ge(y_done, p * GT)
                for f in range(FT):
                    unit(p, v, U_Z + f, ACT.Silu)
                for b in range(GT):
                    n = p * GT + b
                    if not (last and b == GT - 1):
                        decays(n + 1, (b + 1) % GT)
                    act.wait_ge(y_done, n + 1)
                    act.activation(yh[:, :, :], y[:, :, :], ACT.Copy).then_inc(yh_done, 1)
                    if not last and b < 3:
                        piece(p + 1, 1 - v, b)
                if not last:
                    piece(p + 1, 1 - v, 3)

            act.preload_act_table_set(LN_EXP_SET)
            act.wait_ge(const_in, 16 * 7)
            act.activation(neg_a[:, :], neg_a[:, :], ACT.Exp).then_inc(init_done, 1)
            act.sem_inc(unit_read, 2)
            for b in range(GT):
                piece(0, 0, b)
            decays(0, 0)
            groups(act, group)

        @block.vector
        def _(dve):
            def prepare(p):
                x = lambda b: tile_of(p, b)
                norm.dve_stats(dve, p, 0, x)
                dve.wait_ge(norm.turned, p)
                norm.dve_apply(dve, p, 0, x, ln_done)
                dve.wait_ge(ln_done, p + 1)
                for b in range(GT):
                    dve.tensor_tensor(x(b), x(b), norm.xn[:, 0, b * C:(b + 1) * C], ALU.add).then_inc(add_done, 1)
                for b in range(GT):
                    dve.bn_stats(norm.stats[:, 0, b], norm.xn[:, 0, b * C:(b + 1) * C])
                dve.drain()
                for b in range(GT):
                    ins = dve.bn_aggr(mv2[:, b], norm.stats[:, 0, b])
                ins.then_inc(mv2_done, 1)
                dve.wait_ge(mv2_done, p + 1)
                dve.tensor_tensor(ms[:, :], mv2[:, :, 0], mv2[:, :, 0], ALU.mult).then_inc(sq_done, 1)
                dve.wait_ge(sq_done, p + 1)
                dve.tensor_tensor(ms[:, :], ms[:, :], mv2[:, :, 1], ALU.add).then_inc(msum_done, 1)
                dve.wait_ge(msum_done, p + 1)
                dve.tensor_scalar(ms[:, :], ms[:, :], RMS_EPS, None, ALU.add).then_inc(ms_done, 1)
                dve.wait_ge(r2_done, p + 1)
                dve.wait_ge(add_done, GT * (p + 1))
                for b in range(GT):
                    xn = norm.xn[:, 0, b * C:(b + 1) * C]
                    ins = dve.scalar_tensor_tensor(out=xn, in0=xn, scalar=r2[:, b:b + 1], in1=norm_w[:, :],
                                                   op0=ALU.mult, op1=ALU.mult)
                ins.then_inc(norm.xn_done, 1)

            def convolve(p, v, f):
                out = xc[:, v, f]
                for k in range(TAPS):
                    src = xpad[:, f, :, k:k + P]
                    if k == 0:
                        dve.wait_ge(unit_read, 2 + p * UNITS + U_X + f + 1)
                        ins = dve.tensor_scalar(out, src, conv_w[:, f, 0:1], conv_b[:, f:f + 1], ALU.mult, ALU.add)
                    else:
                        dve.wait_ge(conv_step, (p * FT + f) * TAPS + k)
                        ins = dve.scalar_tensor_tensor(out=out, in0=src, scalar=conv_w[:, f, k:k + 1], in1=out,
                                                       op0=ALU.mult, op1=ALU.add)
                    ins.then_inc(conv_step, 1)
                dve.wait_ge(conv_step, (p * FT + f + 1) * TAPS)
                dve.tensor_copy(xpad[:, f, :, 0:TAPS - 1], xpad[:, f, :, P:P + TAPS - 1]).then_inc(halo_done, 1)

            def piece(p, v, b):
                if b == 0:
                    norm.dve_lo(dve, p, 0)
                if b == 1:
                    convolve(p, v, 0)
                    rows = lambda ap: ap.unsqueeze(1).broadcast_to([P, GT, NH])
                    dve.wait_ge(dt_turned, p + 1)
                    dve.tensor_tensor(dt0[:, :, :], ps_dt, rows(dt_bias[:, :]), ALU.add).then_inc(dt0_done, 1)
                    dve.wait_ge(dt0_done, p + 1)
                    flat = lambda ap: ap.rearrange("p b h -> p (b h)")
                    dve.scalar_tensor_tensor(out=flat(dta[:, :, :]), in0=flat(dt0[:, :, :]), scalar=-1.0, in1=flat(dt0[:, :, :]),
                                             op0=ALU.mult, op1=ALU.max).then_inc(dta_done, 1)
                    convolve(p, v, 1)
                    dve.wait_ge(dtl_done, p + 1)
                    dve.scalar_tensor_tensor(out=flat(dt[:, v]), in0=flat(dt0[:, :, :]), scalar=0.0, in1=flat(dta[:, :, :]),
                                             op0=ALU.max, op1=ALU.add).then_inc(dt_done, 1)
                    dve.wait_ge(dt_done, p + 1)
                    dve.tensor_tensor(a[:, :, :], dt[:, v], rows(neg_a[:, :]), ALU.mult).then_inc(a_done, 1)
                if b == 2:
                    convolve(p, v, 2)
                    convolve(p, v, 3)
                if b == 3:
                    dve.wait_ge(cb_done, p + 1)
                    dve.tensor_tensor(cb[:, v], ps_cb, tri[:, :].unsqueeze(1).broadcast_to([P, GT, P]), ALU.mult)\
                        .then_inc(cbm_done, 1)

            def decays(p, v, b):
                r, n = b % 2, p * GT + b
                dve.wait_ge(lb_in[r], (p * (GT // 2) + b // 2 + 1) * 16)
                dve.wait_ge(l_copied, 2 * (p + 1))
                ls = l_tok[:, v, b]
                for h in range(NH):
                    ins = dve.tensor_scalar(dec[:, r, h], lb[:, r, h], ls[:, h:h + 1], 0.0, ALU.subtract, ALU.min)
                ins.then_inc(dsub_done, 1)
                dve.tensor_tensor(edge[:, r, 0], lb[:, r, :, P - 1], ls, ALU.subtract)
                dve.tensor_copy(edge[:, r, 1], lb[:, r, :, P - 1]).then_inc(edge_in, 1)

            def weigh(p, v, b):
                n = p * GT + b
                dve.wait_ge(dexp_done, n + 1)
                dve.wait_ge(cbm_done, p + 1)
                dve.tensor_tensor(dec[:, b % 2], dec[:, b % 2], cb[:, v, b].unsqueeze(1).broadcast_to([P, NH, P]),
                                  ALU.mult).then_inc(w_done, 1)

            def times_dt(p, v, b):
                n = p * GT + b
                dve.wait_ge(x_turned, n + 1)
                dve.tensor_tensor(xdt[:, b % 2], ps_x.rearrange("p (h d) -> p h d", h=NH),
                                  dt[:, v, b].unsqueeze(2).broadcast_to([P, NH, DH]), ALU.mult).then_inc(xdt_done, 1)

            def gate(p, v, b):
                n = p * GT + b
                dve.wait_ge(y_summed, n + 1)
                dve.wait_ge(yl_done, n)
                for f in range(FT):
                    ins = dve.scalar_tensor_tensor(out=y[:, f], in0=xc[:, v, f, b], scalar=d_col[:, f:f + 1],
                                                   in1=ps_y[:, f * P:(f + 1) * P], op0=ALU.mult, op1=ALU.add)
                ins.then_inc(yd_done, 1)
                dve.wait_ge(yd_done, n + 1)
                dve.wait_ge(unit_read, 2 + (p + 1) * UNITS)
                dve.tensor_tensor(y[:, :, :], y[:, :, :], zs[:, :, b], ALU.mult).then_inc(y_done, 1)

            def update_state(p, v, b):
                n = p * GT + b
                dve.wait_ge(edge_done, n + 1)
                dve.tensor_tensor(H[:, b], H[:, b], edge[:, b % 2, 1].unsqueeze(2).broadcast_to([P, NH, DH]),
                                  ALU.mult).then_inc(h_decayed, 1)
                dve.wait_ge(h_decayed, n + 1)
                dve.wait_ge(state_done, n + 1)
                dve.tensor_tensor(H[:, b], H[:, b], ps_h.rearrange("p (h d) -> p h d", h=NH), ALU.add)\
                    .then_inc(h_done, 1)

            def residual(p, b):
                n = p * GT + b
                x = tile_of(p, b)
                dve.wait_ge(out_done, n + 1)
                dve.tensor_tensor(x, x, ps_o, ALU.add).then_inc(x_done, 1)

            def group(p, v, last):
                if not last:
                    prepare(p + 1)
                times_dt(p, v, 0)
                for b in range(GT):
                    weigh(p, v, b)
                    if b:
                        residual(p, b - 1)
                    if b + 1 < GT:
                        decays(p, v, b + 1)
                        times_dt(p, v, b + 1)
                    elif not last:
                        decays(p + 1, 1 - v, 0)
                    gate(p, v, b)
                    update_state(p, v, b)
                    if not last and b < 3:
                        piece(p + 1, 1 - v, b)
                residual(p, GT - 1)
                if not last:
                    piece(p + 1, 1 - v, 3)

            dve.memset(H[:, :, :, :], 0.0).then_inc(h_done, GT)
            for f in range(FT):
                dve.memset(xpad[:, f, :, 0:TAPS - 1], 0.0).then_inc(halo_done, 1)
            dve.wait_ge(const_in, 16 * 7)
            dve.wait_ge(init_done, 1)
            dve.tensor_scalar(neg_a[:, :], neg_a[:, :], -1.0, None, ALU.mult).then_inc(init_done, 3)
            dve.wait_ge(init_done, 4)
            prepare(0)
            for b in range(GT):
                piece(0, 0, b)
            decays(0, 0, 0)
            groups(dve, group)
            dve.wait_ge(x_done, TILES)

        @block.gpsimd
        def _(pool):
            def norms(p):
                norm.pool_rstd(pool, p, 0)
                pool.wait_ge(ms_done, p + 1)
                pool.tensor_tensor(r2[:, :], ms[:, :], norm.power[:, :], ALU.pow).then_inc(r2_done, 1)

            def scale_c(n, v, b):
                pool.wait_ge(e0_done, n + 1)
                if not isinstance(n, int) or n:
                    pool.wait_ge(y_summed, n - 1)
                pool.tensor_tensor(cts[:, b % 2], e0[:, :, :], cT[:, v, b].unsqueeze(1).broadcast_to([P, NH, P]),
                                   ALU.mult).then_inc(cts_done, 1)

            def group(p, v, last):
                if not last:
                    norms(p + 1)
                for b in range(GT):
                    n = p * GT + b
                    pool.wait_ge(xdt_done, n + 1)
                    pool.wait_ge(edge_done, n + 1)
                    pool.wait_ge(state_done, n)
                    pool.tensor_tensor(xd2[:, :, :], xdt[:, b % 2], edge[:, b % 2, 0].unsqueeze(2).broadcast_to([P, NH, DH]),
                                       ALU.mult).then_inc(xd2_done, 1)
                    if b < 3:
                        scale_c(n + 1, v, b + 1)
                    elif not last:
                        scale_c(n + 1, 1 - v, 0)
                    pool.wait_ge(yh_done, n + 1)
                    pool.wait_ge(out_done, n)
                    pool.tensor_tensor(yl[:, :, :], y[:, :, :], f32(yh[:, :, :]), ALU.subtract).then_inc(yl_done, 1)

            norm.pool_setup(pool)
            norms(0)
            scale_c(0, 0, 0)
            groups(pool, group)

        @block.sync
        def _(sp):
            for n, (dst, name) in enumerate(((tri[:, :], "tri"), (conv_w[:, :, :], "conv_w"), (conv_b[:, :], "conv_b"),
                                             (d_col[:, :], "d_col"), (norm_w[:, :], "norm_w"), (dt_bias[:, :], "dt_bias"),
                                             (neg_a[:, :], "a_log"))):
                src = c_dram[name]
                if name in ("norm_w", "dt_bias", "a_log"):
                    src = src.partition_broadcast(P)
                if name == "conv_w":
                    src = src.rearrange("p (f k) -> p f k", f=FT)
                sp.dma_start(dst, src).then_inc(const_in, 16)

            def spread(p, v):
                sp.wait_ge(l_copied, 2 * (p + 1))
                sp.dma_start(decay_dram[v], l_row[:, :]).then_inc(l_stored, 16)
                sp.wait_ge(l_stored, 16 * (p + 1))
                for b in range(GT):
                    n = p * GT + b
                    if isinstance(p, int) and p == 0 and b < 2:
                        pass
                    else:
                        sp.wait_ge(e0_done, n - 1)
                        sp.wait_ge(edge_in, n - 1)
                    sp.dma_start(lb[:, b % 2], decay_dram[v, b * NH:(b + 1) * NH, :].partition_broadcast(P))\
                        .then_inc(lb_in[b % 2], 16)

            spread(0, 0)
            with sp.Fori(0, PT // 2 - 1) as i:
                spread(i * 2 + 1, 1)
                spread(i * 2 + 2, 0)
            spread(PT - 1, 1)
FFN_MATS = ("wf", "wi", "wc", "uf", "ui", "uc", "wo", "uo")
E = 8


def build(nc, t, out, phases="FAFMSM"):
    with ExitStack() as ctx:
        sb = lambda n, s, d: ctx.enter_context(nc.sbuf_tensor(n, s, d))
        X = sb("X", [P, TILES * C], F32)
        ident = sb("ident", [P, P], F32)
        gate_bias = sb("ffn_gate_bias", [P, 3 * KC], F32)
        in_c = sb("ffn_in_c", [P, KC], F32)
        bo_rows = sb("ffn_bo_rows", [P, C], F32)
        gate_b = sb("moe_gate_b", [E, 1], F32)
        expert_b = sb("moe_expert_b", [E, C], F32)
        iota = sb("moe_iota", [P, E], F32)
        neg = sb("neg", [P, P], BF16)
        ident16 = sb("ident16", [P, P], BF16)
        proj_bias = sb("proj_bias", [P, C], F32)
        parts_dram = nc.dram_tensor("qk_parts", (2, PARTS, B * C, T), BF16).ap()
        decay_dram = nc.dram_tensor("decays", (2, GT * NH, P), F32).ap()
        ps = ctx.enter_context(nc.psum_tensor("ps", [P, 8, BANK], F32))

        needs = {"F": {"even": ["ffn_w"]}, "A": {"proj": ["proj_w"], "qkv": ["qkv_w"]},
                 "M": {"experts": ["moe_w", "moe_gate"]}, "S": {"even": ["ssm_w"]}}
        columns = lambda names: sum(t[name].shape[1] for name in names)
        regions, holds = {}, {}

        def open_region(stack, r, width):
            regions[r] = [stack.enter_context(nc.sbuf_tensor(f"w_{r}_{part}", [P, width], F32R)) for part in ("hi", "lo")]

        def weight_jobs(phase):
            jobs = []
            for r, names in needs[phase].items():
                if holds.get(r) != phase:
                    holds[r], at = phase, 0
                    for name in names:
                        w = t[name].shape[1]
                        jobs.append((t[name], *(part[:, at:at + w] for part in regions[r])))
                        at += w
            return jobs

        def weights(r, at, k, m):
            return tuple(part[:, at:at + k * m].rearrange("p (k m) -> p k m", k=k) for part in regions[r])

        open_region(ctx, "even", max(columns(needs["F"]["even"]), columns(needs["S"]["even"]) + FT * P))
        early, mid, late = (ctx.enter_context(ExitStack()) for _ in range(3))
        if "A" in phases:
            open_region(early, "proj", columns(needs["A"]["proj"]))
            V = early.enter_context(nc.sbuf_tensor("v", [P, TILES * C], F32))
            open_region(mid, "qkv", columns(needs["A"]["qkv"]))
        if "M" in phases and "A" not in phases:
            open_region(late, "experts", columns(needs["M"]["experts"]))

        load_phase(nc, X, t["x"], weight_jobs(phases[0]),
                   [(ident[:, :], t["identity"]), (gate_bias[:, :], t["ffn_gate_bias"]), (in_c[:, :], t["ffn_in_c"]),
                    (bo_rows[:, :], t["ffn_bo"].partition_broadcast(P)), (gate_b[:, :], t["moe_gate_b"]),
                    (expert_b[:, :], t["moe_expert_b"]), (iota[:, :], t["iota"]),
                    (proj_bias[:, :], t["proj_b"].partition_broadcast(P))], (t["masks"], neg, ident16))
        for n, (ph, then) in enumerate(zip(phases, phases[1:] + " ")):
            jobs = weight_jobs(then) if then != " " else []
            if ph == "F":
                ffn_phase(nc, f"ffn{n}", X, ident, ps, weights("even", 0, 8 * KC, C), (gate_bias, in_c, bo_rows), jobs,
                          V if "A" in phases[n:] else None)
            if ph == "A":
                assert not jobs
                qkv_phase(nc, f"qkv{n}", X, ident, ps, weights("qkv", 0, KC, 3 * C), V, parts_dram, proj_bias)
                mid.close()
                attention_phase(nc, f"att{n}", ident, ps, V, parts_dram, neg, ident16)
                projection_phase(nc, f"proj{n}", X, ident, ps, weights("proj", 0, KC, C), V)
                early.close()
                if "M" in phases:
                    open_region(late, "experts", columns(needs["M"]["experts"]))
            if ph == "M":
                moe_phase(nc, f"moe{n}", X, ident, ps, (weights("experts", 0, KC, E * C), weights("experts", KC * E * C, KC, E)),
                          (gate_b, expert_b, iota), jobs)
            if ph == "S":
                ssm_phase(nc, f"ssm{n}", X, ident, ps, weights("even", 0, KC, PROJ), weights("even", KC * PROJ, FT, C),
                          weights("even", KC * PROJ + FT * C, FT, P), t, decay_dram)
        store_phase(nc, X, out)


def _rows(w):
    return np.ascontiguousarray(w.reshape(w.shape[0] // P, P, w.shape[1]).transpose(1, 0, 2)).reshape(P, -1)


def layout(d):
    d = {k: np.asarray(v) for k, v in d.items()}
    f = lambda n: d["L0_ffn_" + n]
    cols = lambda v: np.ascontiguousarray(v.reshape(-1, P).T)
    return {
        "x": d["L0_attn_x"],
        "identity": np.eye(P, dtype=np.float32),
        "ffn_w": np.concatenate([_rows(f(n).T) for n in FFN_MATS], axis=1),
        "ffn_gate_bias": np.concatenate([cols(f(n)) for n in ("bf", "bi", "bc")], axis=1),
        "ffn_in_c": cols(f("in_c")),
        "ffn_bo": f("bo"),
        "moe_w": _rows(d["L1_ffn_expert_w"].transpose(2, 0, 1).reshape(C, -1)),
        "moe_gate": _rows(d["L1_ffn_gate_w"].T),
        "moe_gate_b": d["L1_ffn_gate_b"].reshape(-1, 1),
        "moe_expert_b": d["L1_ffn_expert_b"],
        "qkv_w": _rows(d["L0_attn_w_qkv"].T),
        "proj_w": _rows(d["L0_attn_w_proj"].T),
        "proj_b": d["L0_attn_b_proj"],
        "masks": np.triu(np.full((P, P), -1e30, np.float32), 1),
        "ssm_w": np.concatenate([_rows(d["L1_attn_in_proj_w"].T), _rows(d["L1_attn_out_proj_w"].T)], axis=1),
        "tri": np.triu(np.ones((P, P), np.float32)),
        "conv_w": _rows(d["L1_attn_conv_w"]),
        "conv_b": cols(d["L1_attn_conv_b"]),
        "d_col": cols(np.repeat(d["L1_attn_D"], DH)),
        "norm_w": d["L1_attn_norm_w"],
        "dt_bias": d["L1_attn_dt_bias"],
        "a_log": d["L1_attn_A_log"],
        "iota": np.tile(np.arange(8, dtype=np.float32), (P, 1)),
    }


def kernel(**inputs):
    import concourse.bacc as bacc
    from concourse.bass_utils import run_bass_kernel_spmd

    nc = bacc.Bacc("TRN2", target_bir_lowering=False, num_devices=1)
    arrays = {f"in_{name}": np.ascontiguousarray(a) for name, a in layout(inputs).items()}
    tensors = {name[3:]: nc.dram_tensor(name, a.shape, mybir.dt.from_np(a.dtype), kind="ExternalInput").ap()
               for name, a in arrays.items()}
    out = nc.dram_tensor("out", (B, T, C), F32, kind="ExternalOutput").ap()
    build(nc, tensors, out)
    return run_bass_kernel_spmd(nc, [arrays], core_ids=[0]).results[0]["out"]
```

```python
from contextlib import ExitStack

import numpy as np

import concourse.bass as bass
from concourse import mybir

F32 = mybir.dt.float32
F32R = mybir.dt.float32r
BF16 = mybir.dt.bfloat16
U32 = mybir.dt.uint32
ALU = mybir.AluOpType
ACT = mybir.ActivationFunctionType
AX = mybir.AxisListType

P = 128
B, T, C = 4, 1024, 256
KC = C // P
TILES = B * T // P
PT = T // P
GT = 4
GROUPS = TILES // GT
GN = GT * P
GW = GT * C
BANK = 512
LN_EPS = 1e-5
RING = 4

SIGMOID_SET = "sigmoid_and_others"
EXP_SET = "exp_and_others"
LN_EXP_SET = "natural_log_exp_and_others"
SILU_SET = "silu_and_others"


def f32(ap):
    return ap.bitcast(F32)


def matmul3(pe, out, lhs_hi, lhs_lo, rhs_hi, rhs_lo, ks, first=True, last=True):
    passes = [(l, r, k) for k in ks for l, r in ((lhs_hi, rhs_hi), (lhs_lo, rhs_hi), (lhs_hi, rhs_lo))]
    for n, (l, r, k) in enumerate(passes):
        ins = pe.matmul(out, l(k), r(k), start=first and n == 0, stop=last and n == len(passes) - 1)
    return ins


class Phase(ExitStack):

    def __init__(self, nc):
        super().__init__()
        self.nc, self.semaphores = nc, []

    def sem(self, name):
        self.semaphores.append(self.nc.alloc_semaphore(name=name))
        return self.semaphores[-1]

    def __exit__(self, *error):
        super().__exit__(*error)
        if error[0] is None:
            self.nc.clear_and_free_semaphores(self.semaphores)
            self.nc.all_engine_barrier()


class Norm:

    def __init__(self, nc, sb, sem, psum_t, ident, tag, slots=2):
        self.nc, self.ps, self.ident = nc, psum_t, ident
        self.xn = sb(f"{tag}_xn", [P, slots, GW], F32)
        self.stats = sb(f"{tag}_stats", [P, slots, GT, 6], F32)
        self.mv = sb(f"{tag}_mv", [P, slots, GT, 2], F32)
        self.var = sb(f"{tag}_var", [P, slots, GT], F32)
        self.rstd = sb(f"{tag}_rstd", [P, slots, GT], F32)
        self.power = sb(f"{tag}_power", [P, GT], F32)
        self.xh = sb(f"{tag}_xh", [P, slots, KC, GN], F32R)
        self.xl = sb(f"{tag}_xl", [P, slots, KC, GN], F32R)
        self.power_set = sem(f"{tag}_power_set")
        self.mv_done = sem(f"{tag}_mv_done")
        self.var_done = sem(f"{tag}_var_done")
        self.rstd_done = sem(f"{tag}_rstd_done")
        self.xn_done = sem(f"{tag}_xn_done")
        self.turned = sem(f"{tag}_turned")
        self.xh_done = sem(f"{tag}_xh_done")
        self.xl_done = sem(f"{tag}_xl_done")

    def pool_setup(self, pool):
        pool.memset(self.power[:, :], -0.5).then_inc(self.power_set, 1)
        pool.wait_ge(self.power_set, 1)

    def pool_rstd(self, pool, n, s):
        pool.wait_ge(self.var_done, n + 1)
        pool.tensor_tensor(self.rstd[:, s], self.var[:, s], self.power[:, :], ALU.pow).then_inc(self.rstd_done, 1)

    def dve_stats(self, dve, n, s, x):
        for j in range(GT):
            dve.bn_stats(self.stats[:, s, j], x(j))
        dve.drain()
        for j in range(GT):
            ins = dve.bn_aggr(self.mv[:, s, j], self.stats[:, s, j])
        ins.then_inc(self.mv_done, 1)
        dve.wait_ge(self.mv_done, n + 1)
        if not isinstance(n, int) or n:
            dve.wait_ge(self.rstd_done, n)
        dve.tensor_scalar(self.var[:, s], self.mv[:, s, :, 1], LN_EPS, None, ALU.add).then_inc(self.var_done, 1)

    def dve_apply(self, dve, n, s, x, done=None):
        dve.wait_ge(self.rstd_done, n + 1)
        for j in range(GT):
            ins = dve.tensor_scalar(self.xn[:, s, j * C:(j + 1) * C], x(j), self.mv[:, s, j, 0:1],
                                    self.rstd[:, s, j:j + 1], ALU.subtract, ALU.mult)
        ins.then_inc(done or self.xn_done, 1)

    def pe_turn(self, pe, n, s):
        pe.wait_ge(self.xn_done, n + 1)
        pe.wait_ge(self.xh_done, n)
        pe.wait_ge(self.xl_done, n)
        for k in range(KC):
            for j in range(GT):
                ins = pe.transpose(self.ps[:, k, j * P:(j + 1) * P],
                                   self.xn[:, s, j * C + k * P:j * C + (k + 1) * P], self.ident[:, :])
        ins.then_inc(self.turned, 1)

    def act_hi(self, act, n, s):
        act.wait_ge(self.turned, n + 1)
        act.activation(self.xh[:, s], self.ps[:, :, :], ACT.Copy).then_inc(self.xh_done, 1)

    def dve_lo(self, dve, n, s):
        dve.wait_ge(self.xh_done, n + 1)
        dve.tensor_tensor(self.xl[:, s], self.ps[:, :, :], f32(self.xh[:, s]), ALU.subtract).then_inc(self.xl_done, 1)

    def pe_ready(self, pe, n):
        pe.wait_ge(self.xh_done, n + 1)
        pe.wait_ge(self.xl_done, n + 1)


def ffn_phase(nc, tag, X, ident, ps, W, small, jobs=(), hx=None, x_dram=None):
    wh, wl = (part.rearrange("p (m k) c -> p m k c", k=KC) for part in W)
    gate_bias, in_c, bo_rows = small
    HALVES = T // GN
    UNITS = 8
    with Phase(nc) as ctx:
        sb = lambda n, s, d: ctx.enter_context(nc.sbuf_tensor(n, s, d))
        sem = lambda n: ctx.sem(n)
        norm = Norm(nc, sb, sem, ps[:, 0:2], ident, tag)
        gates = sb(f"{tag}_gates", [P, KC, 3, GN], F32)
        c = sb(f"{tag}_c", [P, HALVES, KC, GN], F32)
        ch = sb(f"{tag}_ch", [P, HALVES, KC, GN], F32R)
        cl = sb(f"{tag}_cl", [P, HALVES, KC, GN], F32R)
        hx = hx or sb(f"{tag}_hx", [P, TILES * C], F32)
        hc = sb(f"{tag}_hc", [P, HALVES, GW], F32)
        ring = ps[:, 2:2 + RING]
        unit_done = sem(f"{tag}_unit_done")
        unit_read = sem(f"{tag}_unit_read")
        ig_done = sem(f"{tag}_ig_done")
        fc_done = sem(f"{tag}_fc_done")
        c_done = sem(f"{tag}_c_done")
        ch_done = sem(f"{tag}_ch_done")
        c_split = sem(f"{tag}_c_split")
        hc_ready = sem(f"{tag}_hc_ready")
        hc_done = sem(f"{tag}_hc_done")
        sum_done = [sem(f"{tag}_sum{h}_done") for h in range(HALVES)]
        tanh_done = sem(f"{tag}_tanh_done")
        x_done = sem(f"{tag}_x_done")
        x_in = sem(f"{tag}_x_in")
        split = SplitWeights(nc, sb, sem, tag, jobs)
        block = ctx.enter_context(nc.Block())

        def tile_of(i, h, j):
            return X[:, bass.ds(i * (HALVES * GW) + (h * GT + j) * C, C)]

        def add(eng, i, h):
            cols = hx[:, bass.ds(i * (HALVES * GW) + h * GW, GW)]
            eng.tensor_tensor(cols, cols, hc[:, h], ALU.add).then_inc(sum_done[h], 1)

        @block.tensor
        def _(pe):
            norm.pe_turn(pe, 0, 0)

            def step(i, last):
                for h in range(HALVES):
                    n = i * HALVES + h
                    norm.pe_ready(pe, n)
                    xh = lambda k: norm.xh[:, h, k, :]
                    xl = lambda k: norm.xl[:, h, k, :]
                    for u in range(2 * 3):
                        m, gate = u // 3, u % 3
                        pe.wait_ge(unit_read, n * UNITS + u + 1)
                        out = ring[:, u % RING]
                        w = lambda part, mat: lambda k: part[:, mat, k, m * P:(m + 1) * P]
                        matmul3(pe, out, w(wh, gate), w(wl, gate), xh, xl, range(KC), last=False)
                        pe.wait_ge(c_split, n + 1)
                        matmul3(pe, out, w(wh, 3 + gate), w(wl, 3 + gate), lambda k: ch[:, h, k, :],
                                lambda k: cl[:, h, k, :], range(KC), first=False).then_inc(unit_done, 1)
                        if u == 3 and not (last and h == HALVES - 1):
                            norm.pe_turn(pe, n + 1, (h + 1) % 2)
                    for u in range(6, UNITS):
                        pe.wait_ge(unit_read, n * UNITS + u + 1)
                        for t in range(2):
                            j = (u - 6) * 2 + t
                            ins = matmul3(pe, ring[:, u % RING, t * C:(t + 1) * C],
                                          lambda k: norm.xh[:, h, k, j * P:(j + 1) * P],
                                          lambda k: norm.xl[:, h, k, j * P:(j + 1) * P],
                                          lambda k: wh[:, 6, k, :], lambda k: wl[:, 6, k, :], range(KC))
                        ins.then_inc(unit_done, 1)

            with pe.Fori(0, B - 1) as i:
                step(i, False)
            step(B - 1, True)
            pe.wait_ge(c_split, (B + 1) * HALVES)
            pe.wait_ge(unit_read, RING + GROUPS * UNITS)
            for u in range(PT // 2):
                for t in range(2):
                    h, j = (2 * u + t) // GT, (2 * u + t) % GT
                    ins = matmul3(pe, ring[:, u, t * C:(t + 1) * C],
                                  lambda k: ch[:, h, k, j * P:(j + 1) * P],
                                  lambda k: cl[:, h, k, j * P:(j + 1) * P],
                                  lambda k: wh[:, 7, k, :], lambda k: wl[:, 7, k, :], range(KC))
                ins.then_inc(hc_ready, 1)

        @block.scalar
        def _(act):
            act.preload_act_table_set(SIGMOID_SET)
            act.sem_inc(unit_read, RING)
            norm.act_hi(act, 0, 0)

            def step(i, last):
                for h in range(HALVES):
                    n = i * HALVES + h
                    for u in range(2 * 3):
                        m, gate = u // 3, u % 3
                        if u == 0 or u == 3:
                            act.wait_ge(c_done, 2 * n + 1)
                        act.wait_ge(unit_done, n * UNITS + u + 1)
                        act.activation(gates[:, m, gate], ring[:, u % RING], ACT.Tanh if gate == 2 else ACT.Sigmoid,
                                       bias=gate_bias[:, gate * KC + m:gate * KC + m + 1]).then_inc(unit_read, 1)
                        if u == 4 and not (last and h == HALVES - 1):
                            norm.act_hi(act, n + 1, (h + 1) % 2)
                    for u in range(6, UNITS):
                        act.wait_ge(unit_done, n * UNITS + u + 1)
                        act.activation(hx[:, bass.ds(i * (HALVES * GW) + h * GW + (u - 6) * 2 * C, 2 * C)],
                                       ring[:, u % RING], ACT.Copy).then_inc(unit_read, 1)

            with act.Fori(0, B - 1) as i:
                step(i, False)
            step(B - 1, True)
            with act.Fori(0, B) as i:
                for h in range(HALVES):
                    act.wait_ge(sum_done[h], i + 1)
                    cols = hx[:, bass.ds(i * (HALVES * GW) + h * GW, GW)]
                    act.activation(cols, cols, ACT.Tanh).then_inc(tanh_done, 1)

        @block.vector
        def _(dve):
            for h in range(HALVES):
                for k in range(KC):
                    ins = dve.tensor_copy(c[:, h, k], in_c[:, k:k + 1].broadcast_to([P, GN]))
            ins.then_inc(c_done, 1)
            dve.wait_ge(c_done, 1)
            dve.tensor_copy(ch[:, :, :, :], c[:, :, :, :]).then_inc(ch_done, 1)
            dve.wait_ge(ch_done, 1)
            dve.tensor_tensor(cl[:, :, :, :], c[:, :, :, :], f32(ch[:, :, :, :]), ALU.subtract).then_inc(c_split, 2)
            norm.dve_stats(dve, 0, 0, lambda j: tile_of(0, 0, j))
            norm.dve_apply(dve, 0, 0, lambda j: tile_of(0, 0, j))
            norm.dve_lo(dve, 0, 0)

            def update(n, h, m):
                f, g_in, g = (gates[:, m, q] for q in range(3))
                dve.wait_ge(unit_read, RING + n * UNITS + 3 * m + 3)
                dve.tensor_tensor(g_in, g_in, g, ALU.mult).then_inc(ig_done, 1)
                dve.tensor_tensor(f, f, c[:, h, m], ALU.mult).then_inc(fc_done, 1)
                dve.wait_ge(ig_done, 2 * n + m + 1)
                dve.wait_ge(fc_done, 2 * n + m + 1)
                dve.tensor_tensor(c[:, h, m], f, g_in, ALU.add).then_inc(c_done, 1)

            def step(i, last):
                for h in range(HALVES):
                    n = i * HALVES + h
                    more = not (last and h == HALVES - 1)
                    nxt = lambda j: tile_of(i + (h + 1) // 2, (h + 1) % 2, j)
                    if more:
                        if x_dram is not None and h == HALVES - 1:
                            dve.wait_ge(x_in, (i + 1) * 16)
                        norm.dve_stats(dve, n + 1, (h + 1) % 2, nxt)
                        norm.dve_apply(dve, n + 1, (h + 1) % 2, nxt)
                    update(n, h, 0)
                    if more:
                        norm.dve_lo(dve, n + 1, (h + 1) % 2)
                    update(n, h, 1)
                    dve.wait_ge(c_done, 2 * n + 3)
                    dve.wait_ge(unit_done, n * UNITS + 6)
                    dve.tensor_copy(ch[:, h], c[:, h]).then_inc(ch_done, 1)
                    dve.wait_ge(ch_done, n + 2)
                    dve.tensor_tensor(cl[:, h], c[:, h], f32(ch[:, h]), ALU.subtract).then_inc(c_split, 1)

            with dve.Fori(0, B - 1) as i:
                step(i, False)
            step(B - 1, True)
            for u in range(PT // 2):
                dve.wait_ge(hc_ready, u + 1)
                dve.tensor_tensor(hc[:, u // 2, (u % 2) * BANK:(u % 2 + 1) * BANK].rearrange("p (t c) -> p t c", t=2),
                                  ring[:, u].rearrange("p (t c) -> p t c", t=2),
                                  bo_rows[:, :].unsqueeze(1).broadcast_to([P, 2, C]), ALU.add).then_inc(hc_done, 1)
            dve.wait_ge(hc_done, PT // 2)
            dve.wait_ge(unit_read, RING + GROUPS * UNITS)

            def residual(i, h):
                dve.wait_ge(tanh_done, i * HALVES + h + 1)
                cols = bass.ds(i * (HALVES * GW) + h * GW, GW)
                dve.scalar_tensor_tensor(out=X[:, cols], in0=hx[:, cols], scalar=0.5, in1=X[:, cols],
                                         op0=ALU.mult, op1=ALU.add).then_inc(x_done, 1)

            add(dve, 0, 0)
            with dve.Fori(0, B - 1) as i:
                add(dve, i + 1, 0)
                residual(i, 0)
                residual(i, 1)
            residual(B - 1, 0)
            residual(B - 1, 1)
            dve.wait_ge(x_done, GROUPS)

        @block.gpsimd
        def _(pool):
            norm.pool_setup(pool)
            for s in range(2):
                norm.pool_rstd(pool, s, s)
            with pool.Fori(1, GROUPS // 2) as i:
                for s in range(2):
                    norm.pool_rstd(pool, i * 2 + s, s)
            split.split(pool)
            pool.wait_ge(hc_done, PT // 2)
            pool.wait_ge(unit_read, RING + GROUPS * UNITS)
            with pool.Fori(0, B) as i:
                add(pool, i, HALVES - 1)

        @block.sync
        def _(sp):
            if x_dram is not None:
                x_tiles = X[:, :].rearrange("p (b t c) -> p b t c", b=B, t=PT)
                for b in range(1, B):
                    if b > 1:
                        sp.wait_ge(x_in, 16 * (b - 1))
                    sp.dma_start(x_tiles[:, b], batches(x_dram)[:, b]).then_inc(x_in, 16)
            split.load(sp)


class SplitWeights:

    def __init__(self, nc, sb, sem, tag, jobs, in_flight=2):
        part = lambda ap, a: ap[:, a:min(a + BANK, ap.shape[1])]
        self.jobs = [(part(src, a), part(hi, a), part(lo, a))
                     for src, hi, lo in jobs for a in range(0, src.shape[1], BANK)]
        self.RAW = in_flight
        self.raw = sb(f"{tag}_raw", [P, self.RAW, BANK], F32)
        self.loaded = [sem(f"{tag}_loaded{r}") for r in range(self.RAW)]
        self.hi_done = sem(f"{tag}_w_hi_done")
        self.lo_done = sem(f"{tag}_w_lo_done")

    def load(self, sp):
        for n, (src, _, _) in enumerate(self.jobs):
            if n >= self.RAW:
                sp.wait_ge(self.lo_done, n - self.RAW + 1)
            w = src.shape[1]
            sp.dma_start(self.raw[:, n % self.RAW, 0:w], src).then_inc(self.loaded[n % self.RAW], 16)

    def split(self, eng):
        for n, (src, hi, lo) in enumerate(self.jobs):
            w = src.shape[1]
            raw = self.raw[:, n % self.RAW, 0:w]
            eng.wait_ge(self.loaded[n % self.RAW], 16 * (n // self.RAW + 1))
            eng.tensor_copy(hi, raw).then_inc(self.hi_done, 1)
            eng.wait_ge(self.hi_done, n + 1)
            eng.tensor_tensor(lo, raw, f32(hi), ALU.subtract).then_inc(self.lo_done, 1)
        if self.jobs:
            eng.wait_ge(self.lo_done, len(self.jobs))

    def split_hi(self, act):
        for n, (src, hi, _) in enumerate(self.jobs):
            act.wait_ge(self.loaded[n % self.RAW], 16 * (n // self.RAW + 1))
            act.activation(hi, self.raw[:, n % self.RAW, 0:src.shape[1]], ACT.Copy).then_inc(self.hi_done, 1)

    def split_lo(self, dve):
        for n, (src, hi, lo) in enumerate(self.jobs):
            dve.wait_ge(self.loaded[n % self.RAW], 16 * (n // self.RAW + 1))
            dve.wait_ge(self.hi_done, n + 1)
            dve.tensor_tensor(lo, self.raw[:, n % self.RAW, 0:src.shape[1]], f32(hi), ALU.subtract).then_inc(self.lo_done, 1)
        dve.wait_ge(self.lo_done, len(self.jobs))


def batches(ap):
    return ap.rearrange("b (t p) c -> p b t c", p=P)


def load_phase(nc, X, x_dram, weights, smalls, masks):
    with Phase(nc) as ctx:
        sb = lambda n, s, d: ctx.enter_context(nc.sbuf_tensor(n, s, d))
        sem = lambda n: ctx.sem(n)
        split = SplitWeights(nc, sb, sem, "load", weights, in_flight=8)
        mask_src, neg, ident16 = masks
        mask = sb("load_mask", [P, P], F32)
        small_in = sem("load_small_in")
        consts_done = sem("load_consts_done")
        x_in = sem("load_x_in")
        block = ctx.enter_context(nc.Block())

        @block.sync
        def _(sp):
            split.load(sp)

        @block.scalar
        def _(act):
            act.dma_start(mask[:, :], mask_src).then_inc(small_in, 16)
            for dst, src in smalls:
                act.dma_start(dst, src).then_inc(small_in, 16)
            x_tiles = X[:, :].rearrange("p (b t c) -> p b t c", b=B, t=PT)
            act.dma_start(x_tiles[:, 0], batches(x_dram)[:, 0]).then_inc(x_in, 16)
            split.split_hi(act)
            act.wait_ge(small_in, 16 * (len(smalls) + 1))
            act.wait_ge(x_in, 16)

        @block.vector
        def _(dve):
            dve.wait_ge(small_in, 16 * (len(smalls) + 1))
            dve.tensor_copy(neg[:, :], mask[:, :]).then_inc(consts_done, 1)
            dve.tensor_copy(ident16[:, :], smalls[0][0]).then_inc(consts_done, 1)
            split.split_lo(dve)
            dve.wait_ge(consts_done, 2)


def moe_phase(nc, tag, X, ident, ps, W, small, jobs=(), out=None):
    (eh, el), (gh, gl) = W
    gate_b, expert_b, iota = small
    CHUNKS = E * C // BANK
    with Phase(nc) as ctx:
        sb = lambda n, s, d: ctx.enter_context(nc.sbuf_tensor(f"{tag}_{n}", s, d))
        sem = lambda n: ctx.sem(f"{tag}_{n}")
        norm = Norm(nc, lambda n, s, d: ctx.enter_context(nc.sbuf_tensor(n, s, d)),
                    lambda n: ctx.sem(n), ps[:, 0:2], ident, tag)
        lg = sb("logits", [E, GN], F32)
        top = sb("top", [P, GT], F32)
        ex = sb("exp", [P, GT, E], F32)
        total = sb("total", [P, GT], F32)
        prob = sb("prob", [P, GT, E], F32)
        half = sb("half", [P, GT, E], F32)
        best = sb("best", [P, GT, 8], F32)
        place = sb("place", [P, GT, 8], U32)
        placef = sb("placef", [P, GT, 2], F32)
        pick = sb("pick", [P, 2, GT, E], F32)
        gsel = sb("gsel", [P, 2, GT, E], F32)
        gT = sb("gT", [E, 2, GN], F32)
        ring = ps[:, 2:2 + RING]
        logitsT = ps[0:E, 1, 0:GN]
        logits = ps[:, 0, 0:GT * E].rearrange("p (t e) -> p t e", t=GT)
        gselT = ps[0:E, 6, 0:GN]
        bias = ps[:, 7, 0:C]
        chunk_done = sem("chunk_done")
        lgT_done, lg_done, lt_done = sem("lgT_done"), sem("lg_done"), sem("lt_done")
        top_done, diff_done, exp_done = sem("top_done"), sem("diff_done"), sem("exp_done")
        total_done, rec_done, prob_done = sem("total_done"), sem("rec_done"), sem("prob_done")
        place_done, placef_done = sem("place_done"), sem("placef_done")
        pick_done, both_done, gsel_done = sem("pick_done"), sem("both_done"), sem("gsel_done")
        gT_turned, gT_done = sem("gT_turned"), sem("gT_done")
        bias_done, acc_step = sem("bias_done"), sem("acc_step")
        stored = ctx.sem(f"{tag}_stored")
        split = SplitWeights(nc, lambda n, s, d: ctx.enter_context(nc.sbuf_tensor(n, s, d)),
                             lambda n: ctx.sem(n), tag, jobs)
        block = ctx.enter_context(nc.Block())
        STEPS = GT * (E + 1)
        START = (E, 2 * E + 1, 3 * E + 2, 4 * E + 3)
        tile_of = lambda n, j: X[:, bass.ds(n * GW + j * C, C)]

        @block.tensor
        def _(pe):
            def logits_of(n, s):
                norm.pe_ready(pe, n)
                matmul3(pe, logitsT, lambda k: gh[:, k, :], lambda k: gl[:, k, :],
                        lambda k: norm.xh[:, s, k, :], lambda k: norm.xl[:, s, k, :], range(KC)).then_inc(lgT_done, 1)

            def turn_logits(n):
                for j in range(GT):
                    ins = pe.transpose(logits[:, j], lg[:, j * P:(j + 1) * P], ident[0:E, 0:E])
                ins.then_inc(lt_done, 1)

            def turn_gates(n, s):
                pe.wait_ge(gsel_done, n + 1)
                pe.wait_ge(gT_done, n)
                for j in range(GT):
                    ins = pe.transpose(gselT[:, j * P:(j + 1) * P], gsel[:, s, j], ident[:, :])
                ins.then_inc(gT_turned, 1)

            def experts(n, s, j, first=False, logits_next=None):
                for q in range(CHUNKS):
                    if q == CHUNKS - 1 and logits_next is not None:
                        pe.wait_ge(lg_done, logits_next + 1)
                    if j == 0:
                        pe.wait_ge(acc_step, n * STEPS + (START[3] - STEPS + 2 * q + 2))
                    else:
                        pe.wait_ge(acc_step, n * STEPS + (START[j - 1] + 2 * q + 2 + (first and j == 1)))
                    matmul3(pe, ring[:, q], lambda k: norm.xh[:, s, k, j * P:(j + 1) * P],
                            lambda k: norm.xl[:, s, k, j * P:(j + 1) * P],
                            lambda k: eh[:, k, q * BANK:(q + 1) * BANK],
                            lambda k: el[:, k, q * BANK:(q + 1) * BANK], range(KC)).then_inc(chunk_done, 1)

            def biases(n, s, j, added):
                if j == 0:
                    pe.wait_ge(gT_done, n + 1)
                pe.wait_ge(acc_step, added)
                pe.matmul(bias, gT[:, s, j * P:(j + 1) * P], expert_b[:, :],
                          start=True, stop=True).then_inc(bias_done, 1)

            def group(n, s, first=False, last=False):
                experts(n, s, 0)
                if not first:
                    biases(n - 1, 1 - s, 3, n * STEPS + E)
                turn_gates(n, s)
                if not last:
                    norm.pe_turn(pe, n + 1, 1 - s)
                experts(n, s, 1, first)
                biases(n, s, 0, n * STEPS + START[1])
                if not last:
                    logits_of(n + 1, 1 - s)
                experts(n, s, 2, logits_next=None if last else n + 1)
                biases(n, s, 1, n * STEPS + START[2])
                if not last:
                    turn_logits(n + 1)
                experts(n, s, 3)
                biases(n, s, 2, n * STEPS + START[3])
                if last:
                    biases(n, s, 3, n * STEPS + STEPS + E)

            norm.pe_turn(pe, 0, 0)
            logits_of(0, 0)
            pe.wait_ge(lg_done, 1)
            turn_logits(0)
            group(0, 0, first=True)
            with pe.Fori(0, GROUPS // 2 - 1) as i:
                group(i * 2 + 1, 1)
                group(i * 2 + 2, 0)
            group(GROUPS - 1, 1, last=True)


        @block.scalar
        def _(act):
            act.preload_act_table_set(EXP_SET)

            def prepare(n, s):
                norm.act_hi(act, n, s)
                act.wait_ge(lgT_done, n + 1)
                act.activation(lg[:, :], logitsT, ACT.Identity, bias=gate_b[:, 0:1]).then_inc(lg_done, 1)
                act.wait_ge(diff_done, n + 1)
                act.activation(ex[:, :, :], ex[:, :, :], ACT.Exp).then_inc(exp_done, 1)

            def gates(n, s):
                act.wait_ge(gT_turned, n + 1)
                act.activation(gT[:, s], gselT, ACT.Copy).then_inc(gT_done, 1)

            prepare(0, 0)
            with act.Fori(0, GROUPS // 2 - 1) as i:
                for s in range(2):
                    gates(i * 2 + s, s)
                    prepare(i * 2 + s + 1, 1 - s)
            gates(GROUPS - 2, 0)
            prepare(GROUPS - 1, 1)
            gates(GROUPS - 1, 1)

        @block.vector
        def _(dve):
            def softmax_in(n):
                dve.wait_ge(lt_done, n + 1)
                dve.tensor_reduce(top[:, :], logits, AX.X, ALU.max).then_inc(top_done, 1)
                dve.wait_ge(top_done, n + 1)
                dve.tensor_tensor(ex[:, :, :], logits, top[:, :].unsqueeze(2).broadcast_to([P, GT, E]),
                                  ALU.subtract).then_inc(diff_done, 1)

            def choose(n, s):
                dve.wait_ge(exp_done, n + 1)
                dve.tensor_reduce(total[:, :], ex[:, :, :], AX.X, ALU.add).then_inc(total_done, 1)
                dve.wait_ge(total_done, n + 1)
                dve.reciprocal(total[:, :], total[:, :]).then_inc(rec_done, 1)
                dve.wait_ge(rec_done, n + 1)
                dve.tensor_tensor(prob[:, :, :], ex[:, :, :], total[:, :].unsqueeze(2).broadcast_to([P, GT, E]),
                                  ALU.mult).then_inc(prob_done, 1)
                dve.wait_ge(prob_done, n + 1)
                dve.tensor_scalar(half[:, :, :], prob[:, :, :], 0.5, None, ALU.mult)
                for j in range(GT):
                    dve.max(best[:, j], prob[:, j])
                dve.drain()
                for j in range(GT):
                    ins = dve.max_index(place[:, j], best[:, j], prob[:, j])
                ins.then_inc(place_done, 1)
                dve.wait_ge(place_done, n + 1)
                dve.tensor_copy(placef[:, :, :], place[:, :, 0:2]).then_inc(placef_done, 1)
                dve.wait_ge(placef_done, n + 1)
                for r in range(2):
                    ins = dve.tensor_tensor(pick[:, r], iota[:, :].unsqueeze(1).broadcast_to([P, GT, E]),
                                            placef[:, :, r:r + 1].broadcast_to([P, GT, E]), ALU.is_equal)
                ins.then_inc(pick_done, 1)
                dve.wait_ge(pick_done, n + 1)
                dve.tensor_tensor(pick[:, 0], pick[:, 0], pick[:, 1], ALU.add).then_inc(both_done, 1)
                dve.wait_ge(both_done, n + 1)
                dve.tensor_tensor(gsel[:, s], half[:, :, :], pick[:, 0], ALU.mult).then_inc(gsel_done, 1)
                dve.wait_ge(gsel_done, n + 1)

            def experts(n, s, j, step):
                x = tile_of(n, j)
                for e in range(E):
                    if e % 2 == 0:
                        dve.wait_ge(chunk_done, (n * GT + j) * CHUNKS + e // 2 + 1)
                    if e:
                        dve.wait_ge(acc_step, step + e)
                    ins = dve.scalar_tensor_tensor(out=x, in0=ring[:, e // 2, (e % 2) * C:(e % 2 + 1) * C],
                                                   scalar=gsel[:, s, j, e:e + 1], in1=x, op0=ALU.mult, op1=ALU.add)
                    ins.then_inc(acc_step, 1)
                return step + E

            def biases(n, j, step):
                x = tile_of(n, j)
                dve.wait_ge(bias_done, n * GT + j + 1)
                dve.wait_ge(acc_step, step)
                dve.tensor_tensor(x, x, bias, ALU.add).then_inc(acc_step, 1)
                return step + 1

            def group(n, s, first=False, last=False):
                step = n * STEPS + (E + 1 if first else E)
                nxt = lambda j: tile_of(n + 1, j)
                if not last:
                    norm.dve_stats(dve, n + 1, 1 - s, nxt)
                    norm.dve_apply(dve, n + 1, 1 - s, nxt)
                step = experts(n, s, 0, step)
                if not first:
                    step = biases(n - 1, 3, step)
                if not last:
                    norm.dve_lo(dve, n + 1, 1 - s)
                step = experts(n, s, 1, step)
                step = biases(n, 0, step)
                step = experts(n, s, 2, step)
                step = biases(n, 1, step)
                if not last:
                    softmax_in(n + 1)
                step = experts(n, s, 3, step)
                step = biases(n, 2, step)
                if not last:
                    choose(n + 1, 1 - s)
                else:
                    biases(n, 3, step)

            dve.sem_inc(acc_step, E + 1)
            norm.dve_stats(dve, 0, 0, lambda j: tile_of(0, j))
            norm.dve_apply(dve, 0, 0, lambda j: tile_of(0, j))
            norm.dve_lo(dve, 0, 0)
            softmax_in(0)
            choose(0, 0)
            group(0, 0, first=True)
            with dve.Fori(0, GROUPS // 2 - 1) as i:
                group(i * 2 + 1, 1)
                group(i * 2 + 2, 0)
            group(GROUPS - 1, 1, last=True)
            dve.wait_ge(acc_step, E + GROUPS * STEPS + 1)

        @block.gpsimd
        def _(pool):
            norm.pool_setup(pool)
            for s in range(2):
                norm.pool_rstd(pool, s, s)
            with pool.Fori(1, GROUPS // 2) as i:
                for s in range(2):
                    norm.pool_rstd(pool, i * 2 + s, s)
            split.split(pool)

        @block.sync
        def _(sp):
            split.load(sp)
            if out is not None:
                x_tiles = X[:, :].rearrange("p (n t c) -> p n t c", n=GROUPS, t=GT)
                for n in range(GROUPS):
                    sp.wait_ge(acc_step, (n + 1) * STEPS + (2 * E + 1 if n + 1 < GROUPS else E + 1))
                    b, h = n // (T // GN), n % (T // GN)
                    sp.dma_start(batches(out)[:, b, h * GT:(h + 1) * GT], x_tiles[:, n]).then_inc(stored, 16)
                sp.wait_ge(stored, 16 * GROUPS)


HEADS, HD = 16, C // 16
HG = 4
PARTS = 3
Q_PART = (0, 0, 0, 1, 1, 1, 2, 2)
K_PART = (0, 1, 2, 0, 1, 2, 0, 1)
COPIES = P // HD


def qkv_phase(nc, tag, X, ident, ps, W, V, parts_dram, proj_bias):
    wh, wl = W
    HALVES = T // GN
    QK = 2 * KC
    SCALE = (HD ** -0.5, HD ** -0.5, 1.0, 1.0)
    with Phase(nc) as ctx:
        sb = lambda n, s, d: ctx.enter_context(nc.sbuf_tensor(f"{tag}_{n}", s, d))
        sem = lambda n: ctx.sem(f"{tag}_{n}")
        norm = Norm(nc, lambda n, s, d: ctx.enter_context(nc.sbuf_tensor(n, s, d)),
                    lambda n: ctx.sem(n), ps[:, 0:2], ident, tag)
        part = sb("part", [P, HALVES, QK, PARTS, GN], BF16)
        rest = sb("rest", [P, 2, GN], F32)
        ring = ps[:, 2:2 + RING]
        unit_done, v_done, v_read = sem("unit_done"), sem("v_done"), sem("v_read")
        part0_done, part1_done, part2_done = sem("part0_done"), sem("part1_done"), sem("part2_done")
        rest_done, bias_added = sem("rest_done"), sem("bias_added")
        stored = [sem(f"stored{h}") for h in range(HALVES)]
        block = ctx.enter_context(nc.Block())
        tile_of = lambda i, h, j: X[:, bass.ds(i * (HALVES * GW) + (h * GT + j) * C, C)]

        @block.tensor
        def _(pe):
            norm.pe_turn(pe, 0, 0)

            def step(i, last):
                for h in range(HALVES):
                    n = i * HALVES + h
                    norm.pe_ready(pe, n)
                    for u in range(QK):
                        pe.wait_ge(rest_done, n * QK + u + 1)
                        w = lambda p: lambda k: p[:, k, u * P:(u + 1) * P]
                        matmul3(pe, ring[:, u], w(wh), w(wl), lambda k: norm.xh[:, h, k, :],
                                lambda k: norm.xl[:, h, k, :], range(KC)).then_inc(unit_done, 1)
                        if u == 3 and not (last and h == HALVES - 1):
                            norm.pe_turn(pe, n + 1, (h + 1) % 2)
                    for u in range(2):
                        pe.wait_ge(v_read, 2 * n + u + 1)
                        for t in range(2):
                            j = 2 * u + t
                            ins = matmul3(pe, ps[:, 6 + u, t * C:(t + 1) * C],
                                          lambda k: norm.xh[:, h, k, j * P:(j + 1) * P],
                                          lambda k: norm.xl[:, h, k, j * P:(j + 1) * P],
                                          lambda k: wh[:, k, 2 * C:3 * C], lambda k: wl[:, k, 2 * C:3 * C], range(KC))
                        ins.then_inc(v_done, 1)

            with pe.Fori(0, B - 1) as i:
                step(i, False)
            step(B - 1, True)

        @block.scalar
        def _(act):
            act.sem_inc(v_read, 2)
            norm.act_hi(act, 0, 0)

            def step(i, last):
                for h in range(HALVES):
                    n = i * HALVES + h
                    act.wait_ge(stored[h], 16 * (1 + QK * i))
                    for u in range(QK):
                        act.wait_ge(unit_done, n * QK + u + 1)
                        act.activation(part[:, h, u, 0], ring[:, u], ACT.Copy, scale=SCALE[u]).then_inc(part0_done, 1)
                        if u == 3 and not (last and h == HALVES - 1):
                            norm.act_hi(act, n + 1, (h + 1) % 2)
                        if u:
                            second(n, h, u - 1)
                    second(n, h, QK - 1)
                    for u in range(2):
                        act.wait_ge(v_done, 2 * n + u + 1)
                        v = V[:, bass.ds(i * (PT * C), PT * C)].rearrange("p (g t d) -> p t g d", g=HEADS // HG, t=PT)
                        act.activation(v[:, h * GT + 2 * u:h * GT + 2 * u + 2], ps[:, 6 + u].rearrange(
                            "p (t g d) -> p t g d", t=2, g=HEADS // HG), ACT.Copy).then_inc(v_read, 1)

            def second(n, h, u):
                act.wait_ge(rest_done, RING + n * QK + u + 1)
                act.activation(part[:, h, u, 1], rest[:, u % 2], ACT.Copy).then_inc(part1_done, 1)

            with act.Fori(0, B - 1) as i:
                step(i, False)
            step(B - 1, True)

        @block.vector
        def _(dve):
            dve.sem_inc(rest_done, RING)
            dve.sem_inc(part2_done, 1)
            for h in range(HALVES):
                dve.sem_inc(stored[h], 16)
            norm.dve_stats(dve, 0, 0, lambda j: tile_of(0, 0, j))
            norm.dve_apply(dve, 0, 0, lambda j: tile_of(0, 0, j))
            norm.dve_lo(dve, 0, 0)

            def third(n, h, u):
                dve.wait_ge(part1_done, n * QK + u + 1)
                dve.tensor_tensor(part[:, h, u, 2], rest[:, u % 2], part[:, h, u, 1], ALU.subtract).then_inc(part2_done, 1)

            def step(i, last):
                for h in range(HALVES):
                    n = i * HALVES + h
                    more = not (last and h == HALVES - 1)
                    nxt = lambda j: tile_of(i + (h + 1) // 2, (h + 1) % 2, j)
                    if more:
                        norm.dve_stats(dve, n + 1, (h + 1) % 2, nxt)
                        norm.dve_apply(dve, n + 1, (h + 1) % 2, nxt)
                    for u in range(QK):
                        dve.wait_ge(part0_done, n * QK + u + 1)
                        dve.wait_ge(part2_done, 1 + n * QK + max(0, u - 1))
                        dve.scalar_tensor_tensor(out=rest[:, u % 2], in0=ring[:, u], scalar=SCALE[u],
                                                 in1=part[:, h, u, 0], op0=ALU.mult, op1=ALU.subtract).then_inc(rest_done, 1)
                        if u:
                            third(n, h, u - 1)
                        if u == 3 and more:
                            norm.dve_lo(dve, n + 1, (h + 1) % 2)
                    third(n, h, QK - 1)

            with dve.Fori(0, B - 1) as i:
                step(i, False)
            step(B - 1, True)

        @block.gpsimd
        def _(pool):
            norm.pool_setup(pool)
            rows = proj_bias[:, :].unsqueeze(1).broadcast_to([P, GT, C])

            def bias(n, col):
                pool.wait_ge(norm.xn_done, n + 1)
                x = X[:, bass.ds(col, GW)].rearrange("p (t c) -> p t c", t=GT)
                pool.tensor_tensor(x, x, rows, ALU.add).then_inc(bias_added, 1)

            norm.pool_rstd(pool, 0, 0)
            norm.pool_rstd(pool, 1, 1)
            bias(0, 0)
            with pool.Fori(0, GROUPS // 2 - 1) as i:
                norm.pool_rstd(pool, i * 2 + 2, 0)
                bias(i * 2 + 1, i * (2 * GW) + GW)
                norm.pool_rstd(pool, i * 2 + 3, 1)
                bias(i * 2 + 2, i * (2 * GW) + 2 * GW)
            bias(GROUPS - 1, (GROUPS - 1) * GW)
            pool.wait_ge(bias_added, GROUPS)

        @block.sync
        def _(sp):
            with sp.Fori(0, B) as i:
                for h in range(HALVES):
                    for u in range(QK):
                        sp.wait_ge(part2_done, 1 + (i * HALVES + h) * QK + u + 1)
                        rows = bass.ds(i * C + u % KC * P, P)
                        dst = parts_dram[u // KC, :, rows, h * GN:(h + 1) * GN].rearrange("a r t -> r a t")
                        sp.dma_start(dst, part[:, h, u]).then_inc(stored[h], 16)
            for h in range(HALVES):
                sp.wait_ge(stored[h], 16 * (1 + QK * B))


def attention_phase(nc, tag, ident, ps, V, parts_dram, neg, ident16):
    BLOCKS = T // BANK
    pass_units, pass_steps = [], []
    for qb in range(BLOCKS):
        first = qb * GT
        tiles = [[(kj, 0, 0)] for kj in range(first + 1)]
        tiles += [[(first + 1, 0, P), (first + 3, 3 * P, 3 * P)]]
        for together in tiles:
            at = len(pass_units)
            for pair in range(2):
                pass_units.append([(2 * pair + t, kj, t, c, q0) for t in range(2) for kj, c, q0 in together])
            pass_steps.append((qb, at + 1, [(h, kj, at + h // 2, h % 2, c, q0) for kj, c, q0 in together for h in range(HG)]))
        at = len(pass_units)
        pass_units.append([(h, first + 2, h // 2, h % 2 * 2 * P, 2 * P) for h in range(HG)])
        pass_steps.append((qb, at, [(h, first + 2, at, h // 2, h % 2 * 2 * P, 2 * P) for h in range(HG)]))
    PU, PS = len(pass_units), len(pass_steps)
    NU, NS = 2 * PU, 2 * PS
    BODIES = B * HEADS // HG // 2
    step_end = [s * PU + pass_steps[m][1] for s in range(2) for m in range(PS)]
    step_of = [min(m for m in range(NS) if step_end[m] >= u) for u in range(NU)]
    BLOCK_STEPS = [m for m in range(NS) if m % PS == PS - 1 or pass_steps[m % PS + 1][0] != pass_steps[m % PS][0]]
    BLOCK_UNITS = [step_end[m] for m in BLOCK_STEPS]
    AHEAD = 7
    TURN_LAG, COPY_LAG, OUT_LAG = 4, 7, 9
    SU, WU = 3, 12
    assert NU % SU == 0 and NU % WU == 0
    DVE_SQUARES = 6
    LIMIT = 2.0 ** 60

    def outputs_at(x, ends, n, lag, i, first, stage):
        for k, end in enumerate(ends):
            back, at = divmod(end + lag, n)
            if at == x and not (first and back):
                stage((i - back) * len(ends) + k, i - back, k)

    def outputs_left(ends, n, lag, i, stage):
        for k, end in enumerate(ends):
            if end + lag >= n:
                stage(i * len(ends) + k, i, k)

    by_dve = lambda u: u % DVE_SQUARES == DVE_SQUARES - 1
    dve_count = [sum(by_dve(x) for x in range(u)) for u in range(NU + 1)]
    with Phase(nc) as ctx:
        sb = lambda n, s, d: ctx.enter_context(nc.sbuf_tensor(f"{tag}_{n}", s, d))
        sem = lambda n: ctx.sem(f"{tag}_{n}")
        SQ = sb("q_stack", [P, 2, HG, T], BF16)
        SK = sb("k_stack", [P, 2, HG, T], BF16)
        va = sb("v_ones", [P, 2, PT, HG, 2 * HD], F32)
        Wt = sb("weights", [P, WU, 2, BANK], F32)
        oT = sb("oT", [P, 2, BANK], F32)
        den = sb("den", [P, GT, HG], F32)
        scores = lambda u: ps[:, 2 * (u % SU):2 * (u % SU) + 2]
        O = lambda k: ps[:, 6 + k % 2]
        loaded = [sem(f"loaded{s}") for s in range(2)]
        ones_set, v_copied = sem("ones_set"), sem("v_copied")
        s_done, exp_done, clamp_done, ln_done, max_done = (sem(n) for n in ("s_done", "exp_done", "clamp_done", "ln_done", "max_done"))
        sq_pool, sq_dve, pv_done = sem("sq_pool"), sem("sq_dve"), sem("pv_done")
        oT_done, o_turned, den_done, rec_done, o_done = (sem(n) for n in ("oT_done", "o_turned", "den_done", "rec_done", "o_done"))
        block = ctx.enter_context(nc.Block())

        def load(eng, i, s, which=(0, 1)):
            for q_or_k in which:
                stack, parts = ((SQ, Q_PART), (SK, K_PART))[q_or_k]
                for n, part in enumerate(parts):
                    src = parts_dram[q_or_k, part, bass.ds((i * 2 + s) * (HG * HD), HG * HD), :]
                    eng.dma_start(stack[n * HD:(n + 1) * HD, s],
                                  src.rearrange("(h d) t -> d h t", h=HG)).then_inc(loaded[s], 16)

        @block.tensor
        def _(pe):
            def score_unit(i, u):
                i, u = i + u // NU, u % NU
                s, segments = u // PU, pass_units[u % PU]
                if u % PU == 0:
                    pe.wait_ge(loaded[s], (i + 1) * (16 * 2 * COPIES))
                pe.wait_ge(max_done, i * NU + u + 1)
                for h, kj, t, c, q0 in segments:
                    diagonal = kj // GT == u_block(u)
                    q = u_block(u) * BANK + q0
                    w = segment_width(kj, u_block(u))
                    ins = pe.matmul(scores(u)[:, t, c:c + w], SK[:, s, h, kj * P:(kj + 1) * P],
                                    SQ[:, s, h, q:q + w], start=True, stop=not diagonal)
                    if diagonal:
                        ins = pe.matmul(scores(u)[:, t, c:c + P], neg[:, :], ident16[:, :], start=False, stop=True)
                ins.then_inc(s_done, 1)

            def value_unit(i, u):
                m = step_of[u]
                s, (qb, last, products) = m // PS, pass_steps[m % PS]
                if u % PU == 0:
                    pe.wait_ge(v_copied, 2 * i + s + 1)
                if products[0][1:3] == (0, u % PU):
                    pe.wait_ge(o_done, (i * 2 + s) * BLOCKS + qb + 1)
                if by_dve(u):
                    pe.wait_ge(sq_dve, i * dve_count[NU] + dve_count[u + 1])
                else:
                    pe.wait_ge(sq_pool, i * (NU - dve_count[NU]) + (u + 1 - dve_count[u + 1]))
                for h, kj, unit, t, c, q0 in products:
                    if unit == u % PU:
                        w = segment_width(kj, qb)
                        ins = pe.matmul(O(qb)[h * 2 * HD:(h + 1) * 2 * HD, q0:q0 + w], va[:, s, kj, h],
                                        Wt[:, u % WU, t, c:c + w], start=kj == 0, stop=m in BLOCK_STEPS)
                if last == u % PU:
                    ins.then_inc(pv_done, 1)

            def turn_output(n, i, k):
                pe.wait_ge(oT_done, n + 1)
                for j in range(GT):
                    ins = pe.transpose(O(k)[:, j * P:(j + 1) * P], oT[:, k % 2, j * P:(j + 1) * P], ident[:, :])
                ins.then_inc(o_turned, 1)

            def body(i, first=False, last=False):
                for u in range(NU):
                    if not (last and u + AHEAD >= NU):
                        score_unit(i, u + AHEAD)
                    value_unit(i, u)
                    outputs_at(u, BLOCK_UNITS, NU, TURN_LAG, i, first, turn_output)
                if last:
                    outputs_left(BLOCK_UNITS, NU, TURN_LAG, i, turn_output)

            u_block = lambda u: [qb for qb, end, _ in pass_steps if end >= u % PU][0]
            segment_width = lambda kj, qb: BANK - max(0, kj * P - qb * BANK)
            for u in range(AHEAD):
                score_unit(0, u)
            body(0, first=True)
            with pe.Fori(1, BODIES - 1) as i:
                body(i)
            body(BODIES - 1, last=True)

        @block.scalar
        def _(act):
            act.preload_act_table_set(LN_EXP_SET)

            def exp(i, u):
                i, u = i + u // NU, u % NU
                act.wait_ge(s_done, i * NU + u + 1)
                before = step_of[u - WU] + NS if u >= WU else step_of[u - WU + NU]
                act.wait_ge(pv_done, i * NS + before + 1)
                act.activation(Wt[:, u % WU], scores(u), ACT.Exp).then_inc(exp_done, 1)

            def ln(i, u):
                act.wait_ge(clamp_done, i * NU + u + 1)
                act.activation(Wt[:, u % WU], Wt[:, u % WU], ACT.Ln, bias=1.0).then_inc(ln_done, 1)

            def copy_output(n, i, k):
                act.wait_ge(pv_done, (i + 1) * NS + BLOCK_STEPS[k] + 1)
                act.wait_ge(o_turned, n + 1)
                act.activation(oT[:, k % 2], O(k), ACT.Copy).then_inc(oT_done, 1)

            def body(i, first=False, last=False):
                for u in range(NU):
                    if not (last and u == NU - 1):
                        exp(i, u + 1)
                    ln(i, u)
                    outputs_at(u, BLOCK_UNITS, NU, COPY_LAG, i, first, copy_output)
                if last:
                    outputs_left(BLOCK_UNITS, NU, COPY_LAG, i, copy_output)

            load(act, 0, 0, (1,))
            act.sem_inc(o_turned, 2)
            act.sem_inc(o_done, 2)
            act.sem_inc(pv_done, NS)
            exp(0, 0)
            body(0, first=True)
            with act.Fori(1, BODIES - 1) as i:
                body(i)
            body(BODIES - 1, last=True)

        @block.vector
        def _(dve):
            def clamp(i, u):
                i, u = i + u // NU, u % NU
                dve.wait_ge(exp_done, i * NU + u + 1)
                dve.tensor_scalar(Wt[:, u % WU], Wt[:, u % WU], LIMIT, None, ALU.min).then_inc(clamp_done, 1)

            def softplus(i, u):
                wt = Wt[:, u % WU]
                dve.wait_ge(ln_done, i * NU + u + 1)
                dve.tensor_tensor(wt, scores(u), wt, ALU.max).then_inc(max_done, 1)
                if by_dve(u):
                    dve.wait_ge(max_done, SU + i * NU + u + 1)
                    dve.tensor_tensor(wt, wt, wt, ALU.mult).then_inc(sq_dve, 1)

            def divide_output(n, i, k):
                cells = O(k).rearrange("p (j h d) -> p j h d", j=GT, h=HG)
                dve.wait_ge(o_turned, 2 + n + 1)
                dve.tensor_scalar(den[:, :, :], cells[:, :, :, HD], 1e-9, None, ALU.add).then_inc(den_done, 1)
                dve.wait_ge(den_done, n + 1)
                dve.reciprocal(den[:, :, :], den[:, :, :]).then_inc(rec_done, 1)
                dve.wait_ge(rec_done, n + 1)
                out = V[:, bass.ds((i * 2 + k // BLOCKS) * (PT * HG * HD) + k % BLOCKS * (GT * HG * HD), GT * HG * HD)]
                dve.tensor_tensor(out.rearrange("p (j h d) -> p j h d", j=GT, h=HG), cells[:, :, :, 0:HD],
                                  den[:, :, :].unsqueeze(3).broadcast_to([P, GT, HG, HD]), ALU.mult).then_inc(o_done, 1)

            def body(i, first=False, last=False):
                for u in range(NU):
                    if not (last and u == NU - 1):
                        clamp(i, u + 1)
                    softplus(i, u)
                    outputs_at(u, BLOCK_UNITS, NU, OUT_LAG, i, first, divide_output)
                if last:
                    outputs_left(BLOCK_UNITS, NU, OUT_LAG, i, divide_output)

            dve.sem_inc(max_done, SU)
            clamp(0, 0)
            body(0, first=True)
            with dve.Fori(1, BODIES - 1) as i:
                body(i)
            body(BODIES - 1, last=True)

        @block.gpsimd
        def _(pool):
            pool.memset(va[:, :, :, :, :], 1.0).then_inc(ones_set, 1)
            pool.wait_ge(ones_set, 1)

            def copy_v(i, s, used):
                pool.wait_ge(pv_done, used)
                v = V[:, bass.ds((i * 2 + s) * (PT * HG * HD), PT * HG * HD)]
                pool.tensor_copy(va[:, s, :, :, 0:HD], v.rearrange("p (t h d) -> p t h d", t=PT, h=HG)).then_inc(v_copied, 1)

            def body(i, last=False):
                for u in range(NU):
                    if not by_dve(u):
                        pool.wait_ge(max_done, SU + i * NU + u + 1)
                        pool.tensor_tensor(Wt[:, u % WU], Wt[:, u % WU], Wt[:, u % WU], ALU.mult).then_inc(sq_pool, 1)
                    if u == NU // 3:
                        copy_v(i, 1, (i + 1) * NS)
                    if u == NU * 5 // 6 and not last:
                        copy_v(i + 1, 0, (i + 1) * NS + PS)

            copy_v(0, 0, 0)
            with pool.Fori(0, BODIES - 1) as i:
                body(i)
            body(BODIES - 1, last=True)

        @block.sync
        def _(sp):
            load(sp, 0, 0, (0,))
            load(sp, 0, 1)
            with sp.Fori(1, BODIES) as i:
                for s in range(2):
                    sp.wait_ge(s_done, i * NU + (s - 1) * (NU // 2))
                    load(sp, i, s)


def projection_phase(nc, tag, X, ident, ps, W, V):
    wh, wl = W
    with Phase(nc) as ctx:
        sb = lambda n, s, d: ctx.enter_context(nc.sbuf_tensor(f"{tag}_{n}", s, d))
        sem = lambda n: ctx.sem(f"{tag}_{n}")
        o = sb("o", [P, 2, GT, C], F32)
        oh = sb("oh", [P, 2, KC, GN], F32R)
        ol = sb("ol", [P, 2, KC, GN], F32R)
        turn = ps[:, 0:2]
        o_in, turned, oh_done, ol_done = sem("o_in"), sem("turned"), sem("oh_done"), sem("ol_done")
        y_done, x_done = sem("y_done"), sem("x_done")
        block = ctx.enter_context(nc.Block())
        HALVES = T // GN

        @block.scalar
        def _(act):
            def copy_in(i, h):
                n = i * HALVES + h
                if not isinstance(i, int) or i:
                    act.wait_ge(turned, n - 1)
                v = V[:, bass.ds(i * (PT * C), PT * C)].rearrange("p (g t d) -> p t g d", g=HEADS // HG, t=PT)
                act.activation(o[:, h].rearrange("p t (g d) -> p t g d", g=HEADS // HG),
                               v[:, h * GT:(h + 1) * GT], ACT.Copy).then_inc(o_in, 1)

            def hi(n, h):
                act.wait_ge(turned, n + 1)
                act.activation(oh[:, h], turn, ACT.Copy).then_inc(oh_done, 1)

            copy_in(0, 0)
            copy_in(0, 1)
            with act.Fori(0, B - 1) as i:
                for h in range(HALVES):
                    hi(i * HALVES + h, h)
                    copy_in(i + 1, h)
            for h in range(HALVES):
                hi((B - 1) * HALVES + h, h)

        @block.tensor
        def _(pe):
            def turn_in(n, s):
                pe.wait_ge(o_in, n + 1)
                pe.wait_ge(ol_done, n)
                for k in range(KC):
                    for j in range(GT):
                        ins = pe.transpose(turn[:, k, j * P:(j + 1) * P], o[:, s, j, k * P:(k + 1) * P], ident[:, :])
                ins.then_inc(turned, 1)

            def project(n, s):
                pe.wait_ge(ol_done, n + 1)
                for u in range(2):
                    pe.wait_ge(x_done, 2 * n + u + 1)
                    for t in range(2):
                        j = 2 * u + t
                        ins = matmul3(pe, ps[:, 2 + 2 * s + u, t * C:(t + 1) * C],
                                      lambda k: oh[:, s, k, j * P:(j + 1) * P], lambda k: ol[:, s, k, j * P:(j + 1) * P],
                                      lambda k: wh[:, k, :], lambda k: wl[:, k, :], range(KC))
                    ins.then_inc(y_done, 1)

            turn_in(0, 0)
            with pe.Fori(0, GROUPS // 2 - 1) as i:
                turn_in(i * 2 + 1, 1)
                project(i * 2, 0)
                turn_in(i * 2 + 2, 0)
                project(i * 2 + 1, 1)
            turn_in(GROUPS - 1, 1)
            project(GROUPS - 2, 0)
            project(GROUPS - 1, 1)

        @block.vector
        def _(dve):
            dve.sem_inc(x_done, 4)

            def lo(n, s):
                dve.wait_ge(oh_done, n + 1)
                dve.tensor_tensor(ol[:, s], turn, f32(oh[:, s]), ALU.subtract).then_inc(ol_done, 1)

            def residual(n, s):
                for u in range(2):
                    x = X[:, bass.ds(n * GW + u * 2 * C, 2 * C)]
                    dve.wait_ge(y_done, 2 * n + u + 1)
                    dve.tensor_tensor(x, x, ps[:, 2 + 2 * s + u], ALU.add).then_inc(x_done, 1)

            lo(0, 0)
            with dve.Fori(0, GROUPS // 2 - 1) as i:
                lo(i * 2 + 1, 1)
                residual(i * 2, 0)
                lo(i * 2 + 2, 0)
                residual(i * 2 + 1, 1)
            lo(GROUPS - 1, 1)
            residual(GROUPS - 2, 0)
            residual(GROUPS - 1, 1)
            dve.wait_ge(x_done, 4 + 2 * GROUPS)


DI, NH, DH, DS = 2 * C, 8, 64, P
FT = DI // P
TAPS = 4
RMS_EPS = 1e-6
PROJ = 2 * DI + 2 * DS + NH


def ssm_phase(nc, tag, X, ident, ps, W_in, W_out, spare, consts, decay_dram):
    wh, wl = W_in
    oh, ol = W_out
    c_dram = consts
    with Phase(nc) as ctx:
        sb_ = lambda n, s, d: ctx.enter_context(nc.sbuf_tensor(n, s, d))
        sem_ = lambda n: ctx.sem(n)
        sb = lambda n, s, d=F32: sb_(f"{tag}_{n}", s, d)
        sem = lambda n: sem_(f"{tag}_{n}")
        norm = Norm(nc, sb_, sem_, ps[:, 0:2], ident, tag, slots=1)
        tri = sb("tri", [P, P])
        conv_w, conv_b, d_col = sb("conv_w", [P, FT, TAPS]), sb("conv_b", [P, FT]), sb("d_col", [P, FT])
        norm_w, dt_bias, neg_a = sb("norm_w", [P, C]), sb("dt_bias", [P, NH]), sb("neg_a", [P, NH])
        mv2, ms, r2 = sb("mv2", [P, GT, 2]), sb("ms", [P, GT]), sb("r2", [P, GT])
        xpad = sb("xpad", [P, FT, GT, TAPS - 1 + P])
        xc = sb("xc", [P, 2, FT, GT, P])
        zs = sb("zs", [P, FT, GT, P])
        bT, cT = sb("bT", [P, GT, P]), sb("cT", [P, 2, GT, P])
        b_tm = sb("b_tm", [P, GT, P])
        cb = sb("cb", [P, 2, GT, P])
        dtT = sb("dtT", [NH, GN])
        dt0, dta, dt = sb("dt0", [P, GT, NH]), sb("dta", [P, GT, NH]), sb("dt", [P, 2, GT, NH])
        a = sb("a", [P, GT, NH])
        l_tok = sb("l_tok", [P, 2, GT, NH])
        l_row = sb("l_row", [GT * NH, P])
        lb = sb("lb", [P, 2, NH, P])
        e0 = sb("e0", [P, NH, P])
        dec = sb("dec", [P, 2, NH, P])
        cts = sb("cts", [P, 2, NH, P])
        edge = sb("edge", [P, 2, 2, NH])
        xdt = sb("xdt", [P, 2, NH, DH])
        xd2 = sb("xd2", [P, NH, DH])
        H = sb("H", [P, GT, NH, DH])
        y = sb("y", [P, FT, P])
        yh, yl = spare

        small = ps[:, 4, :]
        ps_dt = small[:, 0:GT * NH].rearrange("p (b h) -> p b h", b=GT)
        ps_lrow = small[0:GT * NH, P:2 * P]
        ps_b = small.rearrange("p (b n) -> p b n", b=GT)
        ps_cb = ps[:, 5].rearrange("p (b n) -> p b n", b=GT)
        ps_x, ps_y, ps_h, ps_o = ps[:, 5], ps[:, 6], ps[:, 7], ps[:, 0, 0:C]
        AHEAD = 2
        NORM_AT, SCALE_AT = 0, 3

        (const_in, ln_done, mv2_done, sq_done, msum_done, ms_done, r2_done, add_done,
         init_done) = (sem(n) for n in ("const_in", "ln_done", "mv2_done", "sq_done", "msum_done",
                                        "ms_done", "r2_done", "add_done", "init_done"))
        (unit_done, unit_read, tap_done, conv_step, halo_done, xc_done, dt_turned, dt0_done, dta_done, dte_done, dtl_done,
         dt_done, a_done, l_done, l_copied, l_stored, b_turned, b_copied, cb_done, cbm_done) = (
            sem(n) for n in ("unit_done", "unit_read", "tap_done", "conv_step", "halo_done", "xc_done", "dt_turned", "dt0_done",
                             "dta_done", "dte_done", "dtl_done", "dt_done", "a_done", "l_done", "l_copied",
                             "l_stored", "b_turned", "b_copied", "cb_done", "cbm_done"))
        lb_in = [sem(f"lb_in{r}") for r in range(2)]
        (dsub_done, edge_in, dexp_done, edge_done, e0_done, w_done, cts_done, x_turned, xdt_done, xd2_done, y_summed,
         yd_done, y_done, yh_done, yl_done, state_done, h_decayed, h_done, out_done, x_done) = (
            sem(n) for n in ("dsub_done", "edge_in", "dexp_done", "edge_done", "e0_done", "w_done", "cts_done",
                             "x_turned", "xdt_done", "xd2_done", "y_summed", "yd_done", "y_done", "yh_done", "yl_done",
                             "state_done", "h_decayed", "h_done", "out_done", "x_done"))
        FREE = 1
        block = ctx.enter_context(nc.Block())

        U_DT, U_B, U_C, U_X, U_Z = 0, 1, 2, 3, 3 + FT
        UNITS = 3 + 2 * FT
        COLS = {U_DT: (2 * DI + 2 * DS, NH), U_B: (2 * DI, DS), U_C: (2 * DI + DS, DS)}
        COLS.update({U_X + f: (DI + f * P, P) for f in range(FT)})
        COLS.update({U_Z + f: (f * P, P) for f in range(FT)})
        unit_bank = lambda u: ps[:, 1 + u % 3]
        tile_of = lambda p, b: X[:, bass.ds(p * C + b * (PT * C), C)]

        def groups(eng, group):
            with eng.Fori(0, PT // 2 - 1) as i:
                group(i * 2, 0, 2)
                group(i * 2 + 1, 1, 2)
            group(PT - 2, 0, 1)
            group(PT - 1, 1, 0)

        @block.tensor
        def _(pe):
            def unit(p, v, u):
                at, m = COLS[u]
                pe.wait_ge(unit_read, p * UNITS + u + 1 + (u < 2))
                matmul3(pe, unit_bank(u)[0:m], lambda k: wh[:, k, at:at + m], lambda k: wl[:, k, at:at + m],
                        lambda k: norm.xh[:, 0, k, :], lambda k: norm.xl[:, 0, k, :], range(KC)).then_inc(unit_done, 1)

            def turn_in(p):
                pe.wait_ge(unit_read, 3 + p * UNITS)
                norm.pe_turn(pe, p, 0)

            def piece(p, v, b):
                if b == 0:
                    norm.pe_ready(pe, p)
                    unit(p, v, U_DT)
                if b == 1:
                    unit(p, v, U_B)
                    unit(p, v, U_C)
                    pe.wait_ge(unit_read, 3 + p * UNITS + U_DT + 1)
                    pe.wait_ge(b_copied, p)
                    unit(p, v, U_X)
                    for t in range(GT):
                        ins = pe.transpose(ps_dt[:, t], dtT[:, t * P:(t + 1) * P], ident[0:NH, 0:NH])
                    ins.then_inc(dt_turned, 1)
                    unit(p, v, U_X + 1)
                    pe.wait_ge(a_done, p + 1)
                    pe.matmul(ps_dt, tri[:, :], a[:, :, :], start=True, stop=True)
                    pe.matmul(ps_lrow, a[:, :, :].rearrange("p b h -> p (b h)"), tri[:, :], start=True, stop=True)\
                        .then_inc(l_done, 1)
                if b == 2:
                    unit(p, v, U_X + 2)
                    unit(p, v, U_X + 3)
                if b == 3:
                    pe.wait_ge(l_copied, 2 * (p + 1))
                    for t in range(GT):
                        ins = pe.transpose(ps_b[:, t], bT[:, t], ident[:, :])
                    ins.then_inc(b_turned, 1)
                    pe.wait_ge(xdt_done, FREE + p * GT)
                    for t in range(GT):
                        ins = pe.matmul(ps_cb[:, t], bT[:, t], cT[:, v, t], start=True, stop=True)
                    ins.then_inc(cb_done, 1)

            def turn_x(p, v, b):
                pe.wait_ge(xc_done, p + 1)
                pe.wait_ge(xdt_done, FREE + p * GT + b)
                if b == 0:
                    pe.wait_ge(cbm_done, p + 1)
                for f in range(FT):
                    ins = pe.transpose(ps_x[:, f * P:(f + 1) * P], xc[:, v, f, b], ident[:, :])
                ins.then_inc(x_turned, 1)

            def tile_y(p, v, b):
                n = p * GT + b
                pe.wait_ge(w_done, n + 1)
                pe.wait_ge(cts_done, n + 1)
                pe.wait_ge(h_done, n + 1)
                pe.wait_ge(y_done, FREE + n)
                for h in range(NH):
                    out = ps_y[h % 2 * DH:(h % 2 + 1) * DH, h // 2 * P:(h // 2 + 1) * P]
                    pe.matmul(out, xdt[:, b % 2, h], dec[:, b % 2, h], start=True, stop=False)
                    ins = pe.matmul(out, H[:, b, h], cts[:, b % 2, h], start=False, stop=True)
                ins.then_inc(y_summed, 1)

            def tile_state(p, v, b):
                n = p * GT + b
                pe.wait_ge(xd2_done, n + 1)
                pe.wait_ge(h_done, GT + n)
                pe.matmul(ps_h, b_tm[:, b], xd2[:, :, :].rearrange("p h d -> p (h d)"), start=True, stop=True)\
                    .then_inc(state_done, 1)

            def tile_out(p, v, b):
                n = p * GT + b
                pe.wait_ge(yl_done, FREE + n + 1)
                pe.wait_ge(x_done, FREE + n)
                matmul3(pe, ps_o, lambda k: yh[:, k], lambda k: yl[:, k], lambda k: oh[:, k], lambda k: ol[:, k],
                        range(FT)).then_inc(out_done, 1)

            def group(p, v, left):
                turn_x(p, v, 0)
                unit(p, v, U_Z + 3)
                turn_x(p, v, 1)
                for b in range(GT):
                    tile_y(p, v, b)
                    if b:
                        tile_out(p, v, b - 1)
                    tile_state(p, v, b)
                    if left and b == 0:
                        pe.wait_ge(x_done, FREE + p * GT)
                        turn_in(p + 1)
                    if b + AHEAD < GT:
                        turn_x(p, v, b + AHEAD)
                    if left:
                        piece(p + 1, 1 - v, b)
                if left:
                    unit(p + 1, 1 - v, U_Z)
                    unit(p + 1, 1 - v, U_Z + 1)
                tile_out(p, v, GT - 1)
                if left:
                    unit(p + 1, 1 - v, U_Z + 2)

            pe.wait_ge(init_done, 4)
            turn_in(0)
            for b in range(GT):
                piece(0, 0, b)
            for f in range(3):
                unit(0, 0, U_Z + f)
            groups(pe, group)

        @block.scalar
        def _(act):
            def unit(p, v, u, func=ACT.Copy):
                act.wait_ge(unit_done, p * UNITS + u + 1)
                bank = unit_bank(u)
                as_tiles = lambda ap: ap.rearrange("p (b t) -> p b t", b=GT)
                if u == U_DT:
                    out, src = dtT[:, :], bank[0:NH]
                elif u == U_B:
                    out, src = bT[:, :, :], as_tiles(bank)
                elif u == U_C:
                    out, src = cT[:, v], as_tiles(bank)
                elif u < U_Z:
                    act.wait_ge(halo_done, p * FT + (u - U_X) + 1)
                    out, src = xpad[:, u - U_X, :, TAPS - 1:], as_tiles(bank)
                else:
                    out, src = zs[:, u - U_Z], as_tiles(bank)
                act.activation(out, src, func).then_inc(unit_read, 1)
                if U_X <= u < U_Z:
                    f = u - U_X
                    act.wait_ge(unit_read, 3 + p * UNITS + u + 1)
                    act.activation(xc[:, v, f], xpad[:, f, :, 0:P], ACT.Identity, bias=conv_b[:, f:f + 1],
                                   scale=conv_w[:, f, 0:1]).then_inc(tap_done, 1)

            def piece(p, v, b):
                if b == 0:
                    unit(p, v, U_DT)
                if b == 1:
                    unit(p, v, U_B)
                    unit(p, v, U_C)
                    unit(p, v, U_X)
                    act.wait_ge(dta_done, p + 1)
                    act.activation(dta[:, :, :], dta[:, :, :], ACT.Exp, scale=-1.0).then_inc(dte_done, 1)
                    act.wait_ge(dte_done, p + 1)
                    act.activation(dta[:, :, :], dta[:, :, :], ACT.Ln, bias=1.0).then_inc(dtl_done, 1)
                    unit(p, v, U_X + 1)
                    act.wait_ge(l_done, p + 1)
                    act.wait_ge(l_stored, 16 * p)
                    act.activation(l_row[:, :], ps_lrow, ACT.Copy).then_inc(l_copied, 1)
                    act.activation(l_tok[:, v], ps_dt, ACT.Copy).then_inc(l_copied, 1)
                if b == 2:
                    unit(p, v, U_X + 2)
                    unit(p, v, U_X + 3)
                if b == 3:
                    act.wait_ge(b_turned, p + 1)
                    act.wait_ge(state_done, p * GT)
                    act.activation(b_tm[:, :, :], ps_b, ACT.Copy).then_inc(b_copied, 1)

            def decays(n, v, b, p):
                r = b % 2
                act.wait_ge(lb_in[r], (p * (GT // 2) + b // 2 + 1) * 16)
                act.wait_ge(l_copied, 2 * (p + 1))
                if not isinstance(n, int) or n > 1:
                    act.wait_ge(y_summed, n - 1)
                for h in range(NH):
                    ins = act.activation(dec[:, r, h], lb[:, r, h], ACT.Relu, bias=l_tok[:, v, b, h:h + 1], scale=-1.0)
                ins.then_inc(dsub_done, 1)
                act.wait_ge(dsub_done, n + 1)
                act.activation(dec[:, r], dec[:, r], ACT.Exp, scale=-1.0).then_inc(dexp_done, 1)
                act.wait_ge(edge_in, n + 1)
                act.activation(edge[:, r], edge[:, r], ACT.Exp).then_inc(edge_done, 1)
                act.wait_ge(cts_done, n)
                act.activation(e0[:, :, :], lb[:, r], ACT.Exp).then_inc(e0_done, 1)

            def group(p, v, left):
                act.wait_ge(conv_step, (p + 1) * FT * (TAPS - 1))
                act.activation(xc[:, v], xc[:, v], ACT.Silu).then_inc(xc_done, 1)
                act.wait_ge(y_done, FREE + p * GT)
                for f in range(FT):
                    unit(p, v, U_Z + f, ACT.Silu)
                act.preload_act_table_set(LN_EXP_SET)
                for b in range(GT):
                    n = p * GT + b
                    act.wait_ge(y_done, FREE + n + 1)
                    act.wait_ge(out_done, FREE + n)
                    act.activation(yh[:, :, :], y[:, :, :], ACT.Copy).then_inc(yh_done, 1)
                    if left and b == 0:
                        norm.act_hi(act, p + 1, 0)
                    if left and b:
                        piece(p + 1, 1 - v, b)
                    if left or b + AHEAD < GT:
                        decays(n + AHEAD, v if b + AHEAD < GT else 1 - v, (b + AHEAD) % GT, p + (b + AHEAD) // GT)
                    if left and b == 0:
                        piece(p + 1, 1 - v, b)

            for free in (xdt_done, y_done, x_done, yl_done, out_done):
                act.sem_inc(free, FREE)
            act.preload_act_table_set(LN_EXP_SET)
            act.wait_ge(const_in, 16 * 7)
            act.activation(neg_a[:, :], neg_a[:, :], ACT.Exp).then_inc(init_done, 1)
            act.sem_inc(unit_read, 3)
            norm.act_hi(act, 0, 0)
            for b in range(GT):
                piece(0, 0, b)
            decays(0, 0, 0, 0)
            decays(1, 0, 1, 0)
            groups(act, group)

        @block.vector
        def _(dve):
            def normalise(p):
                x = lambda b: tile_of(p, b)
                norm.dve_stats(dve, p, 0, x)
                dve.wait_ge(norm.turned, p)
                norm.dve_apply(dve, p, 0, x, ln_done)
                dve.wait_ge(ln_done, p + 1)
                for b in range(GT):
                    dve.bn_stats(norm.stats[:, 0, b], norm.xn[:, 0, b * C:(b + 1) * C])
                dve.drain()
                for b in range(GT):
                    ins = dve.bn_aggr(mv2[:, b], norm.stats[:, 0, b])
                ins.then_inc(mv2_done, 1)
                dve.wait_ge(mv2_done, p + 1)
                dve.tensor_tensor(ms[:, :], mv2[:, :, 0], mv2[:, :, 0], ALU.mult).then_inc(sq_done, 1)
                dve.wait_ge(sq_done, p + 1)
                dve.tensor_tensor(ms[:, :], ms[:, :], mv2[:, :, 1], ALU.add).then_inc(msum_done, 1)
                dve.wait_ge(msum_done, p + 1)
                dve.tensor_scalar(ms[:, :], ms[:, :], RMS_EPS, None, ALU.add).then_inc(ms_done, 1)

            def rms_scale(p):
                dve.wait_ge(r2_done, p + 1)
                dve.wait_ge(add_done, GT * (p + 1))
                for b in range(GT):
                    xn = norm.xn[:, 0, b * C:(b + 1) * C]
                    ins = dve.scalar_tensor_tensor(out=xn, in0=xn, scalar=r2[:, b:b + 1], in1=norm_w[:, :],
                                                   op0=ALU.mult, op1=ALU.mult)
                ins.then_inc(norm.xn_done, 1)

            def convolve(p, v, half):
                base = (p * FT + 2 * half) * (TAPS - 1)
                for k in range(1, TAPS):
                    for n in range(2):
                        f = 2 * half + n
                        out, src = xc[:, v, f], xpad[:, f, :, k:k + P]
                        if k == 1:
                            dve.wait_ge(tap_done, p * FT + f + 1)
                        else:
                            dve.wait_ge(conv_step, base + 2 * (k - 2) + n + 1)
                        ins = dve.scalar_tensor_tensor(out=out, in0=src, scalar=conv_w[:, f, k:k + 1], in1=out,
                                                       op0=ALU.mult, op1=ALU.add)
                        ins.then_inc(conv_step, 1)
                for f in (2 * half, 2 * half + 1):
                    dve.tensor_copy(xpad[:, f, :, 0:TAPS - 1], xpad[:, f, :, P:P + TAPS - 1]).then_inc(halo_done, 1)

            def piece(p, v, b):
                if b == 0:
                    norm.dve_lo(dve, p, 0)
                if b == 1:
                    rows = lambda ap: ap.unsqueeze(1).broadcast_to([P, GT, NH])
                    dve.wait_ge(dt_turned, p + 1)
                    dve.tensor_tensor(dt0[:, :, :], ps_dt, rows(dt_bias[:, :]), ALU.add).then_inc(dt0_done, 1)
                    dve.wait_ge(dt0_done, p + 1)
                    flat = lambda ap: ap.rearrange("p b h -> p (b h)")
                    dve.scalar_tensor_tensor(out=flat(dta[:, :, :]), in0=flat(dt0[:, :, :]), scalar=-1.0, in1=flat(dt0[:, :, :]),
                                             op0=ALU.mult, op1=ALU.max).then_inc(dta_done, 1)
                    dve.wait_ge(dtl_done, p + 1)
                    dve.scalar_tensor_tensor(out=flat(dt[:, v]), in0=flat(dt0[:, :, :]), scalar=0.0, in1=flat(dta[:, :, :]),
                                             op0=ALU.max, op1=ALU.add).then_inc(dt_done, 1)
                    dve.wait_ge(dt_done, p + 1)
                    dve.tensor_tensor(a[:, :, :], dt[:, v], rows(neg_a[:, :]), ALU.mult).then_inc(a_done, 1)
                    convolve(p, v, 0)
                if b == 2:
                    convolve(p, v, 1)
                if b == 3:
                    dve.wait_ge(cb_done, p + 1)
                    dve.tensor_tensor(cb[:, v], ps_cb, tri[:, :].unsqueeze(1).broadcast_to([P, GT, P]), ALU.mult)\
                        .then_inc(cbm_done, 1)

            def decays(p, v, b):
                r = b % 2
                dve.wait_ge(lb_in[r], (p * (GT // 2) + b // 2 + 1) * 16)
                dve.wait_ge(l_copied, 2 * (p + 1))
                ls = l_tok[:, v, b]
                dve.tensor_tensor(edge[:, r, 0], lb[:, r, :, P - 1], ls, ALU.subtract)
                dve.tensor_copy(edge[:, r, 1], lb[:, r, :, P - 1]).then_inc(edge_in, 1)

            def weigh(p, v, b):
                n = p * GT + b
                dve.wait_ge(dexp_done, n + 1)
                dve.wait_ge(cbm_done, p + 1)
                dve.tensor_tensor(dec[:, b % 2], dec[:, b % 2], cb[:, v, b].unsqueeze(1).broadcast_to([P, NH, P]),
                                  ALU.mult).then_inc(w_done, 1)

            def times_dt(p, v, b):
                n = p * GT + b
                dve.wait_ge(x_turned, n + 1)
                dve.tensor_tensor(xdt[:, b % 2], ps_x.rearrange("p (h d) -> p h d", h=NH),
                                  dt[:, v, b].unsqueeze(2).broadcast_to([P, NH, DH]), ALU.mult).then_inc(xdt_done, 1)

            def gate(p, v, b):
                n = p * GT + b
                dve.wait_ge(y_summed, n + 1)
                dve.wait_ge(yl_done, FREE + n)
                for f in range(FT):
                    ins = dve.scalar_tensor_tensor(out=y[:, f], in0=xc[:, v, f, b], scalar=d_col[:, f:f + 1],
                                                   in1=ps_y[:, f * P:(f + 1) * P], op0=ALU.mult, op1=ALU.add)
                ins.then_inc(yd_done, 1)
                dve.wait_ge(yd_done, n + 1)
                dve.wait_ge(unit_read, 3 + (p + 1) * UNITS)
                dve.tensor_tensor(y[:, :, :], y[:, :, :], zs[:, :, b], ALU.mult).then_inc(y_done, 1)

            def update_state(p, v, b):
                n = p * GT + b
                dve.wait_ge(h_decayed, n + 1)
                dve.wait_ge(state_done, n + 1)
                dve.tensor_tensor(H[:, b], H[:, b], ps_h.rearrange("p (h d) -> p h d", h=NH), ALU.add)\
                    .then_inc(h_done, 1)

            def residual(p, b):
                n = p * GT + b
                x = tile_of(p, b)
                dve.wait_ge(out_done, FREE + n + 1)
                dve.tensor_tensor(x, x, ps_o, ALU.add).then_inc(x_done, 1)

            def group(p, v, left):
                times_dt(p, v, 0)
                times_dt(p, v, 1)
                for b in range(GT):
                    if b + 1 < GT:
                        weigh(p, v, b + 1)
                    gate(p, v, b)
                    update_state(p, v, b)
                    if b + AHEAD < GT:
                        times_dt(p, v, b + AHEAD)
                    if b:
                        residual(p, b - 1)
                    if left and b in (0, 2):
                        piece(p + 1, 1 - v, b)
                    if b + AHEAD < GT:
                        decays(p, v, b + AHEAD)
                    elif left:
                        decays(p + 1, 1 - v, (b + AHEAD) % GT)
                    if left and b == 1:
                        piece(p + 1, 1 - v, b)
                    if left == 2 and b == NORM_AT:
                        normalise(p + 2)
                    if left == 2 and b == SCALE_AT:
                        rms_scale(p + 2)
                if left:
                    piece(p + 1, 1 - v, 3)
                    weigh(p + 1, 1 - v, 0)
                residual(p, GT - 1)

            dve.memset(H[:, :, :, :], 0.0).then_inc(h_done, GT)
            for f in range(FT):
                dve.memset(xpad[:, f, :, 0:TAPS - 1], 0.0).then_inc(halo_done, 1)
            normalise(0)
            dve.wait_ge(const_in, 16 * 7)
            dve.wait_ge(init_done, 1)
            dve.tensor_scalar(neg_a[:, :], neg_a[:, :], -1.0, None, ALU.mult).then_inc(init_done, 3)
            dve.wait_ge(init_done, 4)
            rms_scale(0)
            for b in range(GT):
                piece(0, 0, b)
                if b == 0:
                    normalise(1)
                if b == 1:
                    rms_scale(1)
            decays(0, 0, 0)
            decays(0, 0, 1)
            weigh(0, 0, 0)
            groups(dve, group)
            dve.wait_ge(x_done, FREE + TILES)

        @block.gpsimd
        def _(pool):
            def norms(p):
                norm.pool_rstd(pool, p, 0)
                pool.wait_ge(ln_done, p + 1)
                for b in range(GT):
                    x = tile_of(p, b)
                    pool.tensor_tensor(x, x, norm.xn[:, 0, b * C:(b + 1) * C], ALU.add).then_inc(add_done, 1)
                pool.wait_ge(ms_done, p + 1)
                pool.tensor_tensor(r2[:, :], ms[:, :], norm.power[:, :], ALU.pow).then_inc(r2_done, 1)

            def scale_c(n, v, b):
                pool.wait_ge(e0_done, n + 1)
                if not isinstance(n, int) or n:
                    pool.wait_ge(y_summed, n - 1)
                pool.tensor_tensor(cts[:, b % 2], e0[:, :, :], cT[:, v, b].unsqueeze(1).broadcast_to([P, NH, P]),
                                   ALU.mult).then_inc(cts_done, 1)

            def scale_x(n, b):
                pool.wait_ge(xdt_done, FREE + n + 1)
                pool.wait_ge(edge_done, n + 1)
                pool.wait_ge(state_done, n)
                pool.tensor_tensor(xd2[:, :, :], xdt[:, b % 2], edge[:, b % 2, 0].unsqueeze(2).broadcast_to([P, NH, DH]),
                                   ALU.mult).then_inc(xd2_done, 1)

            def decay_state(n, b):
                pool.wait_ge(y_summed, n + 1)
                pool.wait_ge(h_done, n + 1)
                pool.tensor_tensor(H[:, b], H[:, b], edge[:, b % 2, 1].unsqueeze(2).broadcast_to([P, NH, DH]),
                                   ALU.mult).then_inc(h_decayed, 1)

            def group(p, v, left):
                decay_state(p * GT, 0)
                for b in range(GT):
                    n = p * GT + b
                    pool.wait_ge(yh_done, n + 1)
                    pool.wait_ge(out_done, FREE + n)
                    pool.tensor_tensor(yl[:, :, :], y[:, :, :], f32(yh[:, :, :]), ALU.subtract).then_inc(yl_done, 1)
                    if b + 1 < GT:
                        scale_x(n + 1, b + 1)
                    if b == NORM_AT and left == 2:
                        norms(p + 2)
                    if b + 1 < GT:
                        decay_state(n + 1, b + 1)
                    if left or b + AHEAD < GT:
                        scale_c(n + AHEAD, v if b + AHEAD < GT else 1 - v, (b + AHEAD) % GT)
                if left:
                    scale_x(n + 1, 0)

            norm.pool_setup(pool)
            norms(0)
            norms(1)
            scale_c(0, 0, 0)
            scale_c(1, 0, 1)
            scale_x(0, 0)
            groups(pool, group)

        @block.sync
        def _(sp):
            for n, (dst, name) in enumerate(((tri[:, :], "tri"), (conv_w[:, :, :], "conv_w"), (conv_b[:, :], "conv_b"),
                                             (d_col[:, :], "d_col"), (norm_w[:, :], "norm_w"), (dt_bias[:, :], "dt_bias"),
                                             (neg_a[:, :], "a_log"))):
                src = c_dram[name]
                if name in ("norm_w", "dt_bias", "a_log"):
                    src = src.partition_broadcast(P)
                if name == "conv_w":
                    src = src.rearrange("p (f k) -> p f k", f=FT)
                sp.dma_start(dst, src).then_inc(const_in, 16)

            def spread(p, v):
                sp.wait_ge(l_copied, 2 * (p + 1))
                sp.dma_start(decay_dram[v], l_row[:, :]).then_inc(l_stored, 16)
                sp.wait_ge(l_stored, 16 * (p + 1))
                for b in range(GT):
                    n = p * GT + b
                    if isinstance(p, int) and p == 0 and b < 2:
                        pass
                    else:
                        sp.wait_ge(e0_done, n - 1)
                        sp.wait_ge(edge_in, n - 1)
                    sp.dma_start(lb[:, b % 2], decay_dram[v, b * NH:(b + 1) * NH, :].partition_broadcast(P))\
                        .then_inc(lb_in[b % 2], 16)

            spread(0, 0)
            with sp.Fori(0, PT // 2 - 1) as i:
                spread(i * 2 + 1, 1)
                spread(i * 2 + 2, 0)
            spread(PT - 1, 1)
FFN_MATS = ("wf", "wi", "wc", "uf", "ui", "uc", "wo", "uo")
E = 8


def build(nc, t, out, phases="FAFMSM"):
    with ExitStack() as ctx:
        sb = lambda n, s, d: ctx.enter_context(nc.sbuf_tensor(n, s, d))
        X = sb("X", [P, TILES * C], F32)
        ident = sb("ident", [P, P], F32)
        gate_bias = sb("ffn_gate_bias", [P, 3 * KC], F32)
        in_c = sb("ffn_in_c", [P, KC], F32)
        bo_rows = sb("ffn_bo_rows", [P, C], F32)
        gate_b = sb("moe_gate_b", [E, 1], F32)
        expert_b = sb("moe_expert_b", [E, C], F32)
        iota = sb("moe_iota", [P, E], F32)
        neg = sb("neg", [P, P], BF16)
        ident16 = sb("ident16", [P, P], BF16)
        proj_bias = sb("proj_bias", [P, C], F32)
        parts_dram = nc.dram_tensor("qk_parts", (2, PARTS, B * C, T), BF16).ap()
        decay_dram = nc.dram_tensor("decays", (2, GT * NH, P), F32).ap()
        ps = ctx.enter_context(nc.psum_tensor("ps", [P, 8, BANK], F32))

        needs = {"F": {"even": ["ffn_w"]}, "A": {"proj": ["proj_w"], "qkv": ["qkv_w"]},
                 "M": {"experts": ["moe_w", "moe_gate"]}, "S": {"even": ["ssm_w"]}}
        columns = lambda names: sum(t[name].shape[1] for name in names)
        regions, holds = {}, {}

        def open_region(stack, r, width):
            regions[r] = [stack.enter_context(nc.sbuf_tensor(f"w_{r}_{part}", [P, width], F32R)) for part in ("hi", "lo")]

        def weight_jobs(phase):
            jobs = []
            for r, names in needs[phase].items():
                if holds.get(r) != phase:
                    holds[r], at = phase, 0
                    for name in names:
                        w = t[name].shape[1]
                        jobs.append((t[name], *(part[:, at:at + w] for part in regions[r])))
                        at += w
            return jobs

        def weights(r, at, k, m):
            return tuple(part[:, at:at + k * m].rearrange("p (k m) -> p k m", k=k) for part in regions[r])

        open_region(ctx, "even", max(columns(needs["F"]["even"]), columns(needs["S"]["even"]) + FT * P))
        early, mid, late = (ctx.enter_context(ExitStack()) for _ in range(3))
        if "A" in phases:
            open_region(early, "proj", columns(needs["A"]["proj"]))
            V = early.enter_context(nc.sbuf_tensor("v", [P, TILES * C], F32))
            open_region(mid, "qkv", columns(needs["A"]["qkv"]))
        if "M" in phases and "A" not in phases:
            open_region(late, "experts", columns(needs["M"]["experts"]))

        load_phase(nc, X, t["x"], weight_jobs(phases[0]),
                   [(ident[:, :], t["identity"]), (gate_bias[:, :], t["ffn_gate_bias"]), (in_c[:, :], t["ffn_in_c"]),
                    (bo_rows[:, :], t["ffn_bo"].partition_broadcast(P)), (gate_b[:, :], t["moe_gate_b"]),
                    (expert_b[:, :], t["moe_expert_b"]), (iota[:, :], t["iota"]),
                    (proj_bias[:, :], t["proj_b"].partition_broadcast(P))], (t["masks"], neg, ident16))
        for n, (ph, then) in enumerate(zip(phases, phases[1:] + " ")):
            jobs = weight_jobs(then) if then != " " else []
            if ph == "F":
                ffn_phase(nc, f"ffn{n}", X, ident, ps, weights("even", 0, 8 * KC, C), (gate_bias, in_c, bo_rows), jobs,
                          V if "A" in phases[n:] else None,
                          t["x"] if n == 0 else None)
            if ph == "A":
                assert not jobs
                qkv_phase(nc, f"qkv{n}", X, ident, ps, weights("qkv", 0, KC, 3 * C), V, parts_dram, proj_bias)
                mid.close()
                attention_phase(nc, f"att{n}", ident, ps, V, parts_dram, neg, ident16)
                projection_phase(nc, f"proj{n}", X, ident, ps, weights("proj", 0, KC, C), V)
                early.close()
                if "M" in phases:
                    open_region(late, "experts", columns(needs["M"]["experts"]))
            if ph == "M":
                moe_phase(nc, f"moe{n}", X, ident, ps, (weights("experts", 0, KC, E * C), weights("experts", KC * E * C, KC, E)),
                          (gate_b, expert_b, iota), jobs, out if n == len(phases) - 1 else None)
            if ph == "S":
                ssm_phase(nc, f"ssm{n}", X, ident, ps, weights("even", 0, KC, PROJ), weights("even", KC * PROJ, FT, C),
                          weights("even", KC * PROJ + FT * C, FT, P), t, decay_dram)


def _rows(w):
    return np.ascontiguousarray(w.reshape(w.shape[0] // P, P, w.shape[1]).transpose(1, 0, 2)).reshape(P, -1)


def layout(d):
    d = {k: np.asarray(v) for k, v in d.items()}
    f = lambda n: d["L0_ffn_" + n]
    cols = lambda v: np.ascontiguousarray(v.reshape(-1, P).T)
    return {
        "x": d["L0_attn_x"],
        "identity": np.eye(P, dtype=np.float32),
        "ffn_w": np.concatenate([_rows(f(n).T) for n in FFN_MATS], axis=1),
        "ffn_gate_bias": np.concatenate([cols(f(n)) for n in ("bf", "bi", "bc")], axis=1),
        "ffn_in_c": cols(f("in_c")),
        "ffn_bo": f("bo"),
        "moe_w": _rows(d["L1_ffn_expert_w"].transpose(2, 0, 1).reshape(C, -1)),
        "moe_gate": _rows(d["L1_ffn_gate_w"].T),
        "moe_gate_b": d["L1_ffn_gate_b"].reshape(-1, 1),
        "moe_expert_b": d["L1_ffn_expert_b"],
        "qkv_w": _rows(d["L0_attn_w_qkv"].T),
        "proj_w": _rows(d["L0_attn_w_proj"].T),
        "proj_b": d["L0_attn_b_proj"],
        "masks": np.triu(np.full((P, P), -1e30, np.float32), 1),
        "ssm_w": np.concatenate([_rows(d["L1_attn_in_proj_w"].T), _rows(d["L1_attn_out_proj_w"].T)], axis=1),
        "tri": np.triu(np.ones((P, P), np.float32)),
        "conv_w": _rows(d["L1_attn_conv_w"]),
        "conv_b": cols(d["L1_attn_conv_b"]),
        "d_col": cols(np.repeat(d["L1_attn_D"], DH)),
        "norm_w": d["L1_attn_norm_w"],
        "dt_bias": d["L1_attn_dt_bias"],
        "a_log": d["L1_attn_A_log"],
        "iota": np.tile(np.arange(8, dtype=np.float32), (P, 1)),
    }


def kernel(**inputs):
    import concourse.bacc as bacc
    from concourse.bass_utils import run_bass_kernel_spmd

    nc = bacc.Bacc("TRN2", target_bir_lowering=False, num_devices=1)
    arrays = {f"in_{name}": np.ascontiguousarray(a) for name, a in layout(inputs).items()}
    tensors = {name[3:]: nc.dram_tensor(name, a.shape, mybir.dt.from_np(a.dtype), kind="ExternalInput").ap()
               for name, a in arrays.items()}
    out = nc.dram_tensor("out", (B, T, C), F32, kind="ExternalOutput").ap()
    build(nc, tensors, out)
    return run_bass_kernel_spmd(nc, [arrays], core_ids=[0]).results[0]["out"]
```
